# Optimizing a Trainium2 kernel written in Bass

```python
import numpy as np
import jax
import jax.numpy as jnp

def _softmax(x, axis=-1):
    return jax.nn.softmax(x, axis=axis)

def _gelu(x):
    return jax.nn.gelu(x, approximate=True)

def _silu(x):
    return jax.nn.silu(x)

def _sigmoid(x):
    return jax.nn.sigmoid(x)

def _layernorm(x, axis=-1, eps=1e-05):
    m = jnp.mean(x, axis=axis, keepdims=True)
    v = jnp.var(x, axis=axis, keepdims=True)
    return (x - m) / jnp.sqrt(v + eps)

def _scatter_add(tgt, idx, src, axis=0):
    return tgt.at[idx].add(src)

def _segment_sum(src, seg, n):
    return jax.ops.segment_sum(src, seg, n)
kernel_name = 'mk_adj_ffn_d1_adj_r2_c25afa'

def setup_inputs(seed: int=0):
    np.random.seed(seed)
    _w = jnp.asarray

    def _rec_inputs():
        import jax
        import jax.numpy as jnp
        _gk = jax.random.key(seed)
        x = 7.22e-05 + 1 * jax.random.normal(jax.random.fold_in(_gk, 1), (16, 512, 128), jnp.float32)
        _a = jax.random.bernoulli(jax.random.fold_in(_gk, 2), 0.00390625, (512, 512))
        _a = jnp.logical_or(_a, jnp.swapaxes(_a, -1, -2))
        _a = jnp.logical_or(_a, jnp.eye(512, dtype=bool))
        _af = _a.astype(jnp.float32)
        _af = _af * jax.random.uniform(jax.random.fold_in(_gk, 3), (512, 512), jnp.float32, 0.05, 0.000976562)
        adj = _af
        return (x, adj)
    x, adj = _rec_inputs()

    def _L0_gnn_setup():
        import jax, jax.numpy as jnp
        import numpy as np
        N_STEPS = 8
        SPATIAL_SCALE = 1.0
        key = jax.random.key(seed)
        ks = jax.random.split(key, 6)
        B, N, D = (32, 512, 128)
        x = jax.random.normal(ks[0], (B, N, D), dtype=jnp.float32)
        adj_mx = jax.random.uniform(ks[1], (N, N), dtype=jnp.float32) / N
        alpha_train = jnp.ones((N,), dtype=jnp.float32)
        w = jnp.eye(D, dtype=jnp.float32) + 0.01 * jax.random.normal(ks[2], (D, D), dtype=jnp.float32)
        d = jax.random.uniform(ks[3], (D,), dtype=jnp.float32)
        fc_in_w = jax.random.normal(ks[4], (D, D), dtype=jnp.float32) * (1.0 / np.sqrt(D))
        fc_in_b = jnp.zeros((D,), dtype=jnp.float32)
        return {'x': x, 'adj_mx': adj_mx, 'alpha_train': alpha_train, 'w': w, 'd': d, 'fc_in_w': fc_in_w, 'fc_in_b': fc_in_b, 'vt': 0}
    _L0_gnn_all = _L0_gnn_setup()
    _L0_gnn_in = {k: v for k, v in _L0_gnn_all.items() if k in ('alpha_train', 'w', 'd', 'fc_in_w', 'fc_in_b')}
    del _L0_gnn_all

    def _L0_ffn_setup():
        import jax, jax.numpy as jnp
        import numpy as np
        NUM_EXPERTS = 8
        TOP_K = 2
        B, S, D = (8, 4096, 128)

        def _moe(tokens, router_w, w1, b1, w2, b2):
            N = tokens.shape[0]
            E = router_w.shape[0]
            logits = tokens.astype(jnp.float32) @ router_w.astype(jnp.float32).T
            probs = jax.nn.softmax(logits, axis=-1)
            rw, re = jax.lax.top_k(probs, TOP_K)
            if TOP_K > 1:
                rw = rw / jnp.maximum(rw.sum(-1, keepdims=True), 1e-12)
            rw = rw.astype(tokens.dtype)
            combine = jnp.zeros((N, E), tokens.dtype).at[jnp.arange(N)[:, None], re].set(rw)
            out = tokens
            for e in range(E):
                h = jax.nn.gelu(tokens @ w1[e] + b1[e], approximate=False)
                y = h @ w2[e] + b2[e]
                out = out + combine[:, e:e + 1] * y
            return out
        key = jax.random.key(seed)
        ks = jax.random.split(key, 4)
        scale = 1.0 / np.sqrt(D).astype(np.float32)
        return {'input_embeddings': jax.random.normal(ks[0], (B, S, D), jnp.float32), 'router_w': jax.random.normal(ks[1], (NUM_EXPERTS, D), jnp.float32) * scale, 'w1': jax.random.normal(ks[2], (NUM_EXPERTS, D, D), jnp.float32) * scale, 'b1': jnp.zeros((NUM_EXPERTS, D), jnp.float32), 'w2': jax.random.normal(ks[3], (NUM_EXPERTS, D, D), jnp.float32) * scale, 'b2': jnp.zeros((NUM_EXPERTS, D), jnp.float32)}
    _L0_ffn_all = _L0_ffn_setup()
    _L0_ffn_in = {k: v for k, v in _L0_ffn_all.items() if k in ('router_w', 'w1', 'b1', 'w2', 'b2')}
    del _L0_ffn_all
    return {'x': x, 'adj': adj, 'L0_gnn_alpha_train': _L0_gnn_in['alpha_train'], 'L0_gnn_w': _L0_gnn_in['w'], 'L0_gnn_d': _L0_gnn_in['d'], 'L0_gnn_fc_in_w': _L0_gnn_in['fc_in_w'], 'L0_gnn_fc_in_b': _L0_gnn_in['fc_in_b'], 'L0_ffn_router_w': _L0_ffn_in['router_w'], 'L0_ffn_w1': _L0_ffn_in['w1'], 'L0_ffn_b1': _L0_ffn_in['b1'], 'L0_ffn_w2': _L0_ffn_in['w2'], 'L0_ffn_b2': _L0_ffn_in['b2']}

def reference(x, adj, L0_gnn_alpha_train, L0_gnn_w, L0_gnn_d, L0_gnn_fc_in_w, L0_gnn_fc_in_b, L0_ffn_router_w, L0_ffn_w1, L0_ffn_b1, L0_ffn_w2, L0_ffn_b2):
    import jax
    import jax.numpy as jnp

    def _L0_gnn_ref(x, adj_mx, alpha_train, w, d, fc_in_w, fc_in_b, vt):
        import jax, jax.numpy as jnp
        import numpy as np
        N_STEPS = 8
        SPATIAL_SCALE = 1.0
        x0 = jax.lax.stop_gradient(x)
        h = jnp.einsum('bnd,ed->bne', x, fc_in_w) + fc_in_b
        alph = jax.nn.sigmoid(alpha_train)[:, None]
        d_clamped = jnp.clip(d, 0.0, 1.0)
        w_eff = w * d_clamped @ w.T
        dt = jnp.float32(SPATIAL_SCALE / N_STEPS)

        def euler_step(h, _):
            ax = jnp.einsum('nm,bmd->bnd', adj_mx, h)
            f = alph * 0.5 * (ax - h) + h @ w_eff - h + x0
            return (h + dt * f, None)
        h, _ = jax.lax.scan(euler_step, h, None, length=N_STEPS)
        return h

    def _L0_ffn_ref(input_embeddings, router_w, w1, b1, w2, b2):
        import jax, jax.numpy as jnp
        import numpy as np
        NUM_EXPERTS = 8
        TOP_K = 2
        B, S, D = (8, 4096, 128)

        def _moe(tokens, router_w, w1, b1, w2, b2):
            N = tokens.shape[0]
            E = router_w.shape[0]
            logits = tokens.astype(jnp.float32) @ router_w.astype(jnp.float32).T
            probs = jax.nn.softmax(logits, axis=-1)
            rw, re = jax.lax.top_k(probs, TOP_K)
            if TOP_K > 1:
                rw = rw / jnp.maximum(rw.sum(-1, keepdims=True), 1e-12)
            rw = rw.astype(tokens.dtype)
            combine = jnp.zeros((N, E), tokens.dtype).at[jnp.arange(N)[:, None], re].set(rw)
            out = tokens
            for e in range(E):
                h = jax.nn.gelu(tokens @ w1[e] + b1[e], approximate=False)
                y = h @ w2[e] + b2[e]
                out = out + combine[:, e:e + 1] * y
            return out
        b, s, d = input_embeddings.shape
        tokens = input_embeddings.reshape(b * s, d)
        return _moe(tokens, router_w, w1, b1, w2, b2).reshape(b, s, d)
    x = x + _L0_gnn_ref(_layernorm(x, axis=-1), adj, L0_gnn_alpha_train, L0_gnn_w, L0_gnn_d, L0_gnn_fc_in_w, L0_gnn_fc_in_b, 0)
    x = x + _L0_ffn_ref(_layernorm(x, axis=-1), L0_ffn_router_w, L0_ffn_w1, L0_ffn_b1, L0_ffn_w2, L0_ffn_b2)
    return x

_drawn_inputs = setup_inputs


def setup_inputs(seed=0):
    import zlib

    import numpy as np

    out = dict(_drawn_inputs(seed))
    spreads = {'L0_gnn_alpha_train': (1.0, 0.6),
     'L0_gnn_fc_in_b': (0.0, 0.1),
     'L0_ffn_b1': (0.0, 0.446),
     'L0_ffn_b2': (0.0, 0.307)}
    factors = {'adj': 3.03}
    for name, (base, spread) in spreads.items():
        noise = np.random.default_rng([zlib.crc32(name.encode()), seed]).standard_normal(out[name].shape)
        drawn = base * np.exp(spread * noise) if base else spread * noise
        out[name] = jnp.asarray(drawn.astype(out[name].dtype))
    for name, factor in factors.items():
        out[name] = (out[name] * factor).astype(out[name].dtype)
    return out
```

```python
import concourse.bass as bass
from concourse import mybir
from contextlib import ExitStack
from math import comb as binomial

FP32 = mybir.dt.float32
F32R = mybir.dt.float32r
I32 = mybir.dt.int32
ALU = mybir.AluOpType
ACT = mybir.ActivationFunctionType
AX = mybir.AxisListType

P = 128
STEPS = 8
DT = 1.0 / STEPS
EPS = 1e-5
BABY = 3
LAG = 3
RING = 4


def build(nc, x, adj, alpha, w, d, fc_w, fc_b, router_w, w1, b1, w2, b2, out):
    B, N, D = x.shape
    E = router_w.shape[0]
    NT = N // P
    GB = 2
    GROUPS = B // GB
    T = NT * GB
    ITEMS = GB * E
    W = GB * D
    C = 2 * E
    K = STEPS + 1
    assert D == P and K == BABY * BABY and N == 512

    ctx = ExitStack()
    with ctx:
        def sb(name, shape, dt=FP32):
            return ctx.enter_context(nc.sbuf_tensor(name, shape, dt))

        def sem(name):
            return ctx.enter_context(nc.semaphore(name))

        ident = sb("ident", [P, P])
        ident_dt = sb("ident_dt", [P, P])
        rows = sb("rows", [NT + E + 2 + E, P])
        cols = sb("cols", [P, NT + E + 2 + E])
        A_COL, B1_COL, D_COL, FB_COL, RT_COL = 0, NT, NT + E, NT + E + 1, NT + E + 2
        node = sb("node", [P, 6, NT])
        ones_v = sb("ones_v", [P, NT, 2], F32R)
        dclip = sb("dclip", [P, 1])
        w_raw = sb("w_raw", [P, 2, P])
        wT = sb("wT", [P, 2, P])
        LT = sb("LT", [P, BABY, 2, NT, N], F32R)
        M = sb("M", [P, 2, BABY, BABY, D], F32R)
        bias = sb("bias", [P, NT, BABY, D])
        w1s = sb("w1s", [P, 2, E, D], F32R)
        w2s = sb("w2s", [P, 2, E, D], F32R)
        b2_raw = sb("b2_raw", [C, D])
        b2s = sb("b2s", [C, 2, D], F32R)
        rts = sb("rts", [P, C], F32R)
        sel_raw = sb("sel_raw", [C, E, P])
        sel = sb("sel", [C, E, P], F32R)
        rank_i = sb("rank_i", [P, T, E], I32)
        rank = sb("rank", [P, T, E])
        nhalf = sb("nhalf", [P, T])

        xg = sb("xg", [P, NT, GB, D])
        x0 = sb("x0", [P, NT, GB, D])
        x0s = sb("x0s", [P, 2, NT, GB, D], F32R)
        GT = sb("GT", [P, GB, BABY, 2, N], F32R)
        y2s = GT[:, 0, :, :, :].rearrange("p i s n -> p (i s n)")[:, 0:2 * T * D] \
            .rearrange("p (s t b c) -> p s t b c", s=2, t=NT, b=GB)
        y1s = GT[:, 1, :, :, :].rearrange("p i s n -> p (i s n)")[:, 0:2 * T * D] \
            .rearrange("p (s t b c) -> p s t b c", s=2, t=NT, b=GB)
        Q = sb("Q", [P, BABY, NT, GB, D])
        y1 = Q[:, 2]
        w12_raw = Q[:, 0:2].rearrange("p k t b c -> p k (t b) c")
        scr = sb("scr", [P, 3, K, D])
        RP = scr[:, 0]
        SK = scr[:, 1]
        crep = scr[:, 2]
        x1 = scr[:, 0, 0:T, :].rearrange("p (t b) c -> p t b c", b=GB)
        z = scr[:, 1, 0:T, :].rearrange("p (t b) c -> p t b c", b=GB)
        res = scr[:, 2, 0:T, :].rearrange("p (t b) c -> p t b c", b=GB)
        bn = sb("bn", [P, 2, T, 6])
        mv = sb("mv", [P, 2, 3, T])
        ve = sb("ve", [P, 2, T])
        rstd = sb("rstd", [P, 2, T])
        zT = sb("zT", [P, 2, GB, N], F32R)
        rt = sb("rt", [P, 6, T, E])
        rm = sb("rm", [P, 10, T])
        cc = sb("cc", [P, T, C])
        combT = sb("combT", [C, GB, N], F32R)
        work = sb("work", [P, 5, N])
        hid = work[:, 0:2]
        scaled = work[:, 2:5]
        Lnat = work[:, 0:4]
        scs = sb("scs", [P, RING, 2, N], F32R)
        Lns = scs[:, :, :, :].rearrange("p r s n -> p s r n")
        yT = sb("yT", [P, N])
        outs = sb("outs", [P, GB, NT, D])

        bank = [ctx.enter_context(nc.psum_tensor(f"bank{i}", [P, 512], FP32)) for i in range(8)]

        rows_in, w_in, adj_in, w12_in, b2_in = (sem(n) for n in ("rows_in", "w_in", "adj_in", "w12_in", "b2_in"))
        pool_const, pool_own = sem("pool_const"), sem("pool_own")
        rows_t, w_t, cols_ready, sig_exp = sem("rows_t"), sem("w_t"), sem("cols_ready"), sem("sig_exp")
        set_own = sem("set_own")
        lnat_ready, lnat_hi, lnat_lo = sem("lnat_ready"), sem("lnat_hi"), sem("lnat_lo")
        wt_ready, weff_mm = sem("wt_ready"), sem("weff_mm")
        pow_mm, pow_ready = sem("pow_mm"), sem("pow_ready")
        lt_mm, lt_hi, lt_lo = sem("lt_mm"), sem("lt_hi"), sem("lt_lo")
        fr_mm, crep_mm, crep_ready = sem("fr_mm"), sem("crep_mm"), sem("crep_ready")
        m_sum, m_hi, m_lo = sem("m_sum"), sem("m_hi"), sem("m_lo")
        v1_ready, v2_mm, v2_read = sem("v1_ready"), sem("v2_mm"), sem("v2_read")
        wsp_hi, wsp_lo = sem("wsp_hi"), sem("wsp_lo")
        small_ready = sem("small_ready")

        x_in = sem("x_in")
        ln_own = [sem("ln1_own"), sem("ln2_own")]
        ln_ve = [sem("ln1_ve"), sem("ln2_ve")]
        ln_rstd = [sem("ln1_rstd"), sem("ln2_rstd")]
        x0_ready, x0_hi, x0_lo = sem("x0_ready"), sem("x0_hi"), sem("x0_lo")
        x0t_mm, x0t_hi, x0t_lo = sem("x0t_mm"), sem("x0t_hi"), sem("x0t_lo")
        gt_mm, gt_hi, gt_lo = sem("gt_mm"), sem("gt_hi"), sem("gt_lo")
        q_mm, q_ready = sem("q_mm"), sem("q_ready")
        y2_hi, y2_lo = sem("y2_hi"), sem("y2_lo")
        y1_mm, y1_add = sem("y1_mm"), sem("y1_add")
        y1_hi, y1_lo = sem("y1_hi"), sem("y1_lo")
        xq_ready = sem("xq_ready")
        h8_mm, x1_add = sem("h8_mm"), sem("x1_add")
        z_ready, res_ready = sem("z_ready"), sem("res_ready")
        zt_mm, zt_hi, zt_lo = sem("zt_mm"), sem("zt_hi"), sem("zt_lo")
        lg_mm, rt_own, rt_pre, rt_exp, comb_ready = (sem(n) for n in ("lg_mm", "rt_own", "rt_pre", "rt_exp", "comb_ready"))
        ct_mm, ct_copied = sem("ct_mm"), sem("ct_copied")
        up_mm, gelu_done, rep_mm, sc_ready = sem("up_mm"), sem("gelu_done"), sem("rep_mm"), sem("sc_ready")
        sc_hi, sc_lo, down_mm = sem("sc_hi"), sem("sc_lo"), sem("down_mm")
        yt_copied, ot_mm = sem("yt_copied"), sem("ot_mm")
        out_add = sem("out_add")
        out_stored = sem("out_stored")
        LN_OWN = T + 2
        RT_OWN = 22

        GT_BANK = [2, 3, 0, 1]
        Y1_BANK = [2, 3, 0, 1]
        H8_BANK = [4, 5, 6, 7]
        UP_BANK, REP_BANK, SUM_BANK = [4, 5], [6, 7], [0, 1]
        ZT_BANK, OT_BANK, LG_BANK, CT_BANK = [3, 2], [2, 3], 4, [5, 6]

        x_v = x.rearrange("(g b) (t p) c -> g b p t c", b=GB, p=P)
        out_v = out.rearrange("(g b) (t p) c -> g b p t c", b=GB, p=P)

        def of_group(v, g, b):
            return v[bass.ds(g, 1), b, :, :, :].rearrange("o p t c -> p (o t) c")

        block = ctx.enter_context(nc.Block())

        @block.sync
        def _(sp):
            sp.sem_inc(out_add, 1)
            sp.sem_inc(out_stored, 1)
            for k, v in ((B1_COL, b1), (RT_COL, router_w)):
                sp.dma_start(rows[k:k + E, :], v).then_inc(rows_in, 16)
            sp.dma_start(rows[A_COL:A_COL + NT, :], alpha.rearrange("(t p) -> t p", p=P)).then_inc(rows_in, 16)
            for k, v in ((D_COL, d), (FB_COL, fc_b)):
                sp.dma_start(rows[k:k + 1, :], v.rearrange("(o p) -> o p", o=1)).then_inc(rows_in, 16)
            sp.dma_start(w_raw[:, 0, :], w).then_inc(w_in, 16)
            sp.dma_start(w_raw[:, 1, :], fc_w).then_inc(w_in, 16)

            def load_x(g):
                for b in range(GB):
                    sp.dma_start(xg[:, :, b, :], of_group(x_v, g, b)).then_inc(x_in, 16)

            def store(h):
                for b in range(GB):
                    sp.wait_ge(out_add, 1 + GB * h + b + 1)
                    sp.dma_start(of_group(out_v, h, b), outs[:, b, :, :]).then_inc(out_stored, 16)

            load_x(0)
            sp.dma_start(w12_raw[:, 0], w1.rearrange("e c f -> c e f")).then_inc(w12_in, 16)
            sp.dma_start(w12_raw[:, 1], w2.rearrange("e f c -> f e c")).then_inc(w12_in, 16)
            for r in (0, E):
                sp.dma_start(b2_raw[r:r + E, :], b2).then_inc(b2_in, 16)

            def iteration(g, first=False, last=False):
                if not last:
                    sp.wait_ge(xq_ready, g + 1)
                    load_x(g + 1)
                if not first:
                    store(g - 1)

            iteration(0, first=True)
            with sp.Fori(1, GROUPS - 1) as g:
                iteration(g)
            iteration(GROUPS - 1, last=True)
            store(GROUPS - 1)
            sp.wait_ge(out_stored, 1 + 32 * GROUPS)

        @block.gpsimd
        def _(pool):
            nc.gpsimd.memset(ident[:, :], 0.0).then_inc(pool_own, 1)
            pool.wait_ge(pool_own, 1)
            nc.gpsimd.affine_select(out=ident[:, :], in_=ident[:, :], compare_op=ALU.not_equal, fill=1.0,
                                    base=0, pattern=[[-1, P]], channel_multiplier=1).then_inc(pool_const, 1)
            nc.gpsimd.memset(sel_raw[:, :, :], 0.0).then_inc(pool_own, 1)
            for r in range(2):
                pool.wait_ge(pool_own, 2 + r)
                nc.gpsimd.affine_select(out=sel_raw[:, :, :], in_=sel_raw[:, :, :], compare_op=ALU.not_equal,
                                        fill=1.0, base=-r * E, pattern=[[-1, E], [0, P]],
                                        channel_multiplier=1).then_inc(pool_own, 1)
            nc.gpsimd.iota(rank_i[:, :, :], pattern=[[0, T], [-1, E]], base=E, channel_multiplier=0)
            nc.gpsimd.memset(nhalf[:, :], -0.5).then_inc(pool_own, 1)
            pool.wait_ge(pool_own, 5)
            nc.gpsimd.tensor_copy(rank[:, :, :], rank_i[:, :, :]).then_inc(pool_const, 1)

            def inverse_root(n, g):
                pool.wait_ge(ln_ve[n], g + 1)
                nc.gpsimd.tensor_tensor(rstd[:, n, :], ve[:, n, :], nhalf[:, :], ALU.pow).then_inc(ln_rstd[n], 1)

            def low_x0(g):
                pool.wait_ge(x0_hi, g + 1)
                nc.gpsimd.tensor_tensor(x0s[:, 1], x0[:, :, :, :], x0s[:, 0].bitcast(FP32),
                                        ALU.subtract).then_inc(x0_lo, 1)

            def item_low(h, i):
                pool.wait_ge(sc_hi, ITEMS * h + i + 1)
                nc.gpsimd.tensor_tensor(scs[:, i % RING, 1, :], scaled[:, i % 3, :],
                                        scs[:, i % RING, 0, :].bitcast(FP32), ALU.subtract).then_inc(sc_lo, 1)

            def residual(h):
                pool.wait_ge(z_ready, h + 1)
                pool.wait_ge(out_add, 1 + GB * h)
                nc.gpsimd.tensor_tensor(res, x1, z, ALU.add).then_inc(res_ready, 1)

            inverse_root(0, 0)
            low_x0(0)
            for k in range(2):
                pool.wait_ge(wsp_hi, k + 1)
                nc.gpsimd.tensor_tensor((w1s, w2s)[k][:, 1], w12_raw[:, k],
                                        (w1s, w2s)[k][:, 0].bitcast(FP32), ALU.subtract).then_inc(wsp_lo, 1)

            def iteration(g, first=False, last=False):
                if not first:
                    residual(g - 1)
                pool.wait_ge(q_ready, T * g + T)
                nc.gpsimd.tensor_tensor(Q[:, 0], Q[:, 0], xg[:, :, :, :], ALU.add).then_inc(xq_ready, 1)
                if not last:
                    inverse_root(0, g + 1)
                    low_x0(g + 1)
                if first:
                    inverse_root(1, g)
                else:
                    for i in range(ITEMS):
                        item_low(g - 1, i)
                        if i == 3:
                            inverse_root(1, g)

            iteration(0, first=True)
            with pool.Fori(1, GROUPS - 1) as g:
                iteration(g)
            iteration(GROUPS - 1, last=True)
            residual(GROUPS - 1)
            for i in range(ITEMS):
                item_low(GROUPS - 1, i)

        @block.scalar
        def _(act):
            act.dma_start(Lnat, adj.rearrange("(t p) m -> p t m", p=P)).then_inc(adj_in, 16)

            def high(dst, src):
                return nc.scalar.activation(dst, src, ACT.Copy)

            act.wait_ge(cols_ready, 1)
            nc.scalar.activation(node[:, 0, :], cols[:, A_COL:A_COL + NT], ACT.Exp, scale=-1.0).then_inc(sig_exp, 1)

            def high_x0(g):
                act.wait_ge(x0_ready, g + 1)
                high(x0s[:, 0], x0[:, :, :, :]).then_inc(x0_hi, 1)

            act.wait_ge(lnat_ready, 1)
            high(Lns[:, 0], Lnat).then_inc(lnat_hi, 1)
            for k in range(BABY):
                for a in range(NT):
                    act.wait_ge(lt_mm, NT * k + a + 1)
                    high(LT[:, k, 0, a, :], bank[4 + a][:, :]).then_inc(lt_hi, 1)
                if k == 0:
                    high_x0(0)
                if k == 1:
                    act.wait_ge(w12_in, 32)
                    high(w1s[:, 0], w12_raw[:, 0]).then_inc(wsp_hi, 1)
                    high(w2s[:, 0], w12_raw[:, 1]).then_inc(wsp_hi, 1)
                    act.wait_ge(pool_own, 5)
                    high(sel[:, :, :], sel_raw[:, :, :]).then_inc(small_ready, 1)
            act.wait_ge(m_sum, BABY)
            high(M[:, 0], SK.rearrange("p (j i) c -> p j i c", i=BABY)).then_inc(m_hi, 1)

            def copy_sum(h, b):
                act.wait_ge(down_mm, ITEMS * h + E * (b + 1))
                if b:
                    act.wait_ge(ot_mm, GB * h + b)
                high(yT[:, :], bank[SUM_BANK[b]][:, :]).then_inc(yt_copied, 1)

            def high_z(g, b):
                act.wait_ge(zt_mm, GB * g + b + 1)
                high(zT[:, 0, b, :], bank[ZT_BANK[b]][:, :]).then_inc(zt_hi, 1)

            def route_exp(h):
                act.wait_ge(rt_pre, h + 1)
                nc.scalar.activation(rt[:, 1], rt[:, 0], ACT.Exp).then_inc(rt_exp, 1)

            def copy_comb(h):
                for b in range(GB):
                    act.wait_ge(ct_mm, GB * h + b + 1)
                    high(combT[:, b, :], bank[CT_BANK[b]][0:C, :]).then_inc(ct_copied, 1)

            def item_high(h, i):
                act.wait_ge(sc_ready, ITEMS * h + i + 1)
                if i >= RING:
                    act.wait_ge(down_mm, ITEMS * h + i - RING + 1)
                high(scs[:, i % RING, 0, :], scaled[:, i % 3, :]).then_inc(sc_hi, 1)

            def experts(h, g=None):
                for i in range(ITEMS):
                    act.wait_ge(up_mm, ITEMS * h + i + 1)
                    if i >= 2:
                        act.wait_ge(sc_ready, ITEMS * h + i - 1)
                    e = i % E
                    nc.scalar.activation(hid[:, i % 2, :], bank[UP_BANK[i % 2]][:, :], ACT.Gelu,
                                         bias=cols[:, B1_COL + e:B1_COL + e + 1]).then_inc(gelu_done, 1)
                    if i >= 1:
                        item_high(h, i - 1)
                    if i == E + LAG:
                        copy_sum(h, 0)
                    if i == E + 6 and g is not None:
                        high_z(g, 0)
                item_high(h, ITEMS - 1)
                if g is not None:
                    high_z(g, 1)
                copy_sum(h, 1)

            def iteration(g, first=False, last=False):
                for b in range(GB):
                    act.wait_ge(x0t_mm, GB * g + b + 1)
                    high(GT[:, b, 0, 0, :], bank[b][:, :]).then_inc(x0t_hi, 1)
                for k in range(2 * GB):
                    if k == 3 and not first:
                        route_exp(g - 1)
                    act.wait_ge(gt_mm, 2 * GB * g + k + 1)
                    high(GT[:, k // 2, 1 + k % 2, 0, :], bank[GT_BANK[k]][:, :]).then_inc(gt_hi, 1)
                for p in range(2):
                    act.wait_ge(q_ready, T * g + NT + 2 * p + 2)
                    high(y2s[:, 0, 2 * p:2 * p + 2], Q[:, 2, 2 * p:2 * p + 2]).then_inc(y2_hi, 1)
                if not first:
                    copy_comb(g - 1)
                for p in range(2):
                    act.wait_ge(y1_add, NT * g + 2 * p + 2)
                    high(y1s[:, 0, 2 * p:2 * p + 2], y1[:, 2 * p:2 * p + 2]).then_inc(y1_hi, 1)
                if not last:
                    high_x0(g + 1)
                if first:
                    for b in range(GB):
                        high_z(g, b)
                else:
                    experts(g - 1, g)

            iteration(0, first=True)
            with act.Fori(1, GROUPS - 1) as g:
                iteration(g)
            iteration(GROUPS - 1, last=True)
            route_exp(GROUPS - 1)
            copy_comb(GROUPS - 1)
            experts(GROUPS - 1)

        @block.vector
        def _(dve):
            v = nc.vector

            def low(dst, src, hi):
                return v.tensor_tensor(dst, src, hi.bitcast(FP32), ALU.subtract)

            def ln_stats(n, g, src, t):
                v.bn_stats(bn[:, n, t, :], src[:, t // GB, t % GB, :]).then_inc(ln_own[n], 1)

            def ln_var(n, g):
                mean_e, mean_o = bn[:, n, :, 1], bn[:, n, :, 4]
                dve.wait_ge(ln_own[n], LN_OWN * g + T)
                v.tensor_tensor(mv[:, n, 1, :], mean_e, mean_o, ALU.subtract)
                v.tensor_tensor(mv[:, n, 2, :], bn[:, n, :, 2], bn[:, n, :, 5], ALU.add)
                v.tensor_tensor(mv[:, n, 0, :], mean_e, mean_o, ALU.add).then_inc(ln_own[n], 1)
                dve.wait_ge(ln_own[n], LN_OWN * g + T + 1)
                v.tensor_tensor(mv[:, n, 1, :], mv[:, n, 1, :], mv[:, n, 1, :], ALU.mult)
                v.tensor_scalar(mv[:, n, 0, :], mv[:, n, 0, :], 0.5, None, ALU.mult)
                v.tensor_scalar(mv[:, n, 2, :], mv[:, n, 2, :], 1.0 / D, EPS, ALU.mult, ALU.add).then_inc(ln_own[n], 1)
                dve.wait_ge(ln_own[n], LN_OWN * g + T + 2)
                v.scalar_tensor_tensor(out=ve[:, n, :], in0=mv[:, n, 1, :], scalar=0.25, in1=mv[:, n, 2, :],
                                       op0=ALU.mult, op1=ALU.add).then_inc(ln_ve[n], 1)

            def ln_scale(n, dst, src, t):
                return v.tensor_scalar(dst[:, t // GB, t % GB, :], src[:, t // GB, t % GB, :],
                                       mv[:, n, 0, t:t + 1], rstd[:, n, t:t + 1], ALU.subtract, ALU.mult)

            def norm_x(g):
                dve.wait_ge(x_in, 32 * g + 32)
                for t in range(T):
                    ln_stats(0, g, xg, t)
                ln_var(0, g)
                dve.wait_ge(ln_rstd[0], g + 1)
                for t in range(T):
                    last = ln_scale(0, x0, xg, t)
                last.then_inc(x0_ready, 1)

            own = [0]

            def step(ins):
                own[0] += 1
                ins.then_inc(set_own, 1)
                dve.wait_ge(set_own, own[0])

            dve.wait_ge(rows_t, 1)
            v.tensor_copy(cols[:, :], bank[0][:, 0:NT + E + 2 + E]).then_inc(cols_ready, 1)
            dve.wait_ge(cols_ready, 1)
            step(v.tensor_scalar(dclip[:, :], cols[:, D_COL:D_COL + 1], 0.0, 1.0, ALU.max, ALU.min))
            dve.wait_ge(w_t, 1)
            v.tensor_copy(wT[:, 0, :], bank[1][:, 0:P])
            v.tensor_scalar(wT[:, 1, :], bank[1][:, 0:P], dclip[:, :], None, ALU.mult).then_inc(wt_ready, 1)
            dve.wait_ge(sig_exp, 1)
            step(v.tensor_scalar(node[:, 1, :], node[:, 0, :], 1.0, None, ALU.add))
            step(v.reciprocal(node[:, 2, :], node[:, 1, :]))
            step(v.tensor_scalar(node[:, 3, :], node[:, 2, :], DT * 0.5, None, ALU.mult))
            step(v.tensor_scalar(node[:, 0, :], node[:, 3, :], -1.0, 1.0 - DT, ALU.mult, ALU.add))
            dve.wait_ge(adj_in, 16)
            dve.wait_ge(pool_const, 1)
            for t in range(NT):
                last = v.tensor_scalar(Lnat[:, t, :], Lnat[:, t, :], node[:, 3, t:t + 1], None, ALU.mult)
            step(last)
            for t in range(NT):
                diag = Lnat[:, t, t * P:(t + 1) * P]
                last = v.scalar_tensor_tensor(out=diag, in0=ident[:, :], scalar=node[:, 0, t:t + 1],
                                              in1=diag, op0=ALU.mult, op1=ALU.add)
            last.then_inc(lnat_ready, 1)
            norm_x(0)
            dve.wait_ge(lnat_hi, 1)
            low(Lns[:, 1], Lnat, Lns[:, 0]).then_inc(lnat_lo, 1)
            step(v.tensor_reduce(node[:, 4, :], Lnat, AX.X, ALU.add))
            step(v.tensor_copy(ones_v[:, :, 0], node[:, 4, :]))
            low(ones_v[:, :, 1], node[:, 4, :], ones_v[:, :, 0]).then_inc(v1_ready, 1)

            def low_lt(k, a):
                dve.wait_ge(lt_hi, NT * k + a + 1)
                low(LT[:, k, 1, a, :], bank[4 + a][:, :], LT[:, k, 0, a, :]).then_inc(lt_lo, 1)

            for a in range(NT):
                low_lt(0, a)
            v.tensor_copy(RP[:, 0, :], ident[:, :])
            v.tensor_scalar(ident_dt[:, :], ident[:, :], DT, None, ALU.mult)
            dve.wait_ge(weff_mm, 1)
            v.tensor_scalar(RP[:, 1, :], bank[2][:, 0:P], DT, None, ALU.mult).then_inc(pow_ready, 1)
            dve.wait_ge(pow_mm, 1)
            v.tensor_copy(RP[:, 2, :], bank[3][:, 0:P]).then_inc(pow_ready, 1)
            dve.wait_ge(pow_mm, 2)
            v.tensor_copy(RP[:, 3:5, :], bank[2][:, 0:2 * P].rearrange("p (k c) -> p k c", c=P)).then_inc(pow_ready, 1)
            dve.wait_ge(pow_mm, 3)
            v.tensor_copy(RP[:, 5:9, :], bank[3][:, :].rearrange("p (k c) -> p k c", c=P)).then_inc(pow_ready, 1)
            for a in range(NT):
                low_lt(1, a)
            step(v.tensor_copy(rts[:, 0:E], cols[:, RT_COL:RT_COL + E]))
            low(rts[:, E:C], cols[:, RT_COL:RT_COL + E], rts[:, 0:E])
            dve.wait_ge(b2_in, 32)
            step(v.tensor_copy(b2s[:, 0, :], b2_raw[:, :]))
            low(b2s[:, 1, :], b2_raw[:, :], b2s[:, 0, :]).then_inc(small_ready, 1)
            for c in range(BABY):
                dve.wait_ge(crep_mm, c + 1)
                for r in range(BABY):
                    k = STEPS - (BABY * c + r)
                    last = v.tensor_scalar(crep[:, k, :], bank[c][:, r * D:(r + 1) * D],
                                           float(binomial(STEPS, k)), None, ALU.mult)
                last.then_inc(crep_ready, 1)
            dve.wait_ge(v2_mm, 1)
            v.tensor_reduce(node[:, 5, :], bank[3][:, 0:2 * NT].rearrange("p (t s) -> p t s", s=2),
                            AX.X, ALU.add).then_inc(v2_read, 1)
            dve.wait_ge(v2_read, 1)
            dve.wait_ge(pow_ready, 4)
            for i in range(1, STEPS):
                for k in range(STEPS - i):
                    last = v.scalar_tensor_tensor(out=SK[:, k, :], in0=RP[:, i, :], scalar=DT * binomial(k + i, i),
                                                  in1=ident_dt[:, :] if i == 1 else SK[:, k, :],
                                                  op0=ALU.mult, op1=ALU.add)
                step(last)
            for c in range(BABY):
                dve.wait_ge(fr_mm, c + 1)
                for r in range(BABY):
                    k = STEPS - (BABY * c + r)
                    src = bank[c][:, r * D:(r + 1) * D]
                    if k == STEPS:
                        last = v.tensor_copy(SK[:, k, :], src)
                    else:
                        last = v.scalar_tensor_tensor(out=SK[:, k, :], in0=src, scalar=float(binomial(STEPS, k)),
                                                      in1=ident_dt[:, :] if k == STEPS - 1 else SK[:, k, :],
                                                      op0=ALU.mult, op1=ALU.add)
                last.then_inc(m_sum, 1)
            cj = crep.rearrange("p (j i) c -> p j i c", i=BABY)
            for i in (1, 2):
                for t in range(NT):
                    last = v.scalar_tensor_tensor(out=bias[:, t], in0=cj[:, :, i, :], scalar=node[:, 3 + i, t:t + 1],
                                                  in1=cj[:, :, 0, :] if i == 1 else bias[:, t],
                                                  op0=ALU.mult, op1=ALU.add)
                step(last)
            dve.wait_ge(m_hi, 1)
            low(M[:, 1], SK.rearrange("p (j i) c -> p j i c", i=BABY), M[:, 0]).then_inc(m_lo, 1)
            for a in range(NT):
                low_lt(2, a)

            def route(h):
                cnt = [0]

                def step(ins):
                    cnt[0] += 1
                    ins.then_inc(rt_own, 1)
                    dve.wait_ge(rt_own, RT_OWN * h + cnt[0])

                def per_token(k):
                    return rm[:, k, :].unsqueeze(2).to_broadcast([P, T, E])

                def before_exp():
                    dve.wait_ge(lg_mm, h + 1)
                    lg = bank[LG_BANK][:, 0:T * C].rearrange("p (t s e) -> p t e s", s=2, e=E)
                    step(v.tensor_reduce(rt[:, 2], lg, AX.X, ALU.add))
                    step(v.tensor_reduce(rm[:, 0, :], rt[:, 2], AX.X, ALU.max))
                    v.tensor_tensor(rt[:, 0], rt[:, 2], per_token(0), ALU.subtract).then_inc(rt_pre, 1)

                def first_largest(prob, mark, k):
                    step(v.tensor_reduce(rm[:, k, :], prob, AX.X, ALU.max))
                    step(v.tensor_tensor(rt[:, 5], prob, per_token(k), ALU.is_equal))
                    step(v.tensor_tensor(rt[:, 5], rt[:, 5], rank[:, :, :], ALU.mult))
                    step(v.tensor_reduce(rm[:, 9, :], rt[:, 5], AX.X, ALU.max))
                    return v.tensor_tensor(mark, rt[:, 5], per_token(9), ALU.is_equal)

                def after_exp():
                    dve.wait_ge(rt_exp, h + 1)
                    step(v.tensor_reduce(rm[:, 1, :], rt[:, 1], AX.X, ALU.add))
                    step(v.reciprocal(rm[:, 2, :], rm[:, 1, :]))
                    step(v.tensor_tensor(rt[:, 0], rt[:, 1], per_token(2), ALU.mult))
                    step(first_largest(rt[:, 0], rt[:, 3], 3))
                    step(v.scalar_tensor_tensor(out=rt[:, 2], in0=rt[:, 3], scalar=-2.0, in1=rt[:, 0],
                                                op0=ALU.mult, op1=ALU.add))
                    step(first_largest(rt[:, 2], rt[:, 4], 4))
                    v.tensor_tensor(rt[:, 3], rt[:, 3], rt[:, 4], ALU.add)
                    step(v.tensor_tensor(rm[:, 5, :], rm[:, 3, :], rm[:, 4, :], ALU.add))
                    step(v.tensor_scalar(rm[:, 6, :], rm[:, 5, :], 1e-12, None, ALU.max))
                    step(v.reciprocal(rm[:, 7, :], rm[:, 6, :]))
                    step(v.tensor_tensor(rt[:, 5], rt[:, 3], rt[:, 0], ALU.mult))
                    step(v.tensor_tensor(rt[:, 4], rt[:, 5], per_token(7), ALU.mult))
                    step(v.tensor_copy(cc[:, :, 0:E].bitcast(F32R), rt[:, 4]))
                    v.tensor_tensor(cc[:, :, E:C], rt[:, 4], cc[:, :, 0:E], ALU.subtract).then_inc(comb_ready, 1)
                    assert cnt[0] == RT_OWN, cnt[0]

                return before_exp, after_exp

            def low_z(g, b):
                dve.wait_ge(zt_hi, GB * g + b + 1)
                low(zT[:, 1, b, :], bank[ZT_BANK[b]][:, :], zT[:, 0, b, :]).then_inc(zt_lo, 1)

            def add_out(h, b):
                dve.wait_ge(ot_mm, GB * h + b + 1)
                dve.wait_ge(res_ready, h + 1)
                dve.wait_ge(out_stored, 1 + 32 * h)
                v.tensor_tensor(outs[:, b, :, :], bank[OT_BANK[b]][:, :].rearrange("p (t c) -> p t c", c=D),
                                res[:, :, b, :], ALU.add).then_inc(out_add, 1)

            def scale_item(h, i):
                dve.wait_ge(gelu_done, ITEMS * h + i + 1)
                dve.wait_ge(rep_mm, ITEMS * h + i + 1)
                if i >= 3:
                    dve.wait_ge(sc_lo, ITEMS * h + i - 2)
                v.tensor_tensor(scaled[:, i % 3, :], hid[:, i % 2, :], bank[REP_BANK[i % 2]][:, :],
                                ALU.mult).then_inc(sc_ready, 1)

            def norm_x1(g, part):
                if part < 4:
                    if part == 0:
                        dve.wait_ge(x1_add, NT * g + NT)
                    for t in (2 * part, 2 * part + 1):
                        ln_stats(1, g, x1, t)
                elif part == 4:
                    ln_var(1, g)
                elif part < 10:
                    if part == 6:
                        dve.wait_ge(ln_rstd[1], g + 1)
                    if part >= 6:
                        for t in (2 * (part - 6), 2 * (part - 6) + 1):
                            last = ln_scale(1, z, x1, t)
                        if part == 9:
                            last.then_inc(z_ready, 1)

            def experts(h, g=None):
                for i in range(ITEMS):
                    scale_item(h, i)
                    if g is not None:
                        norm_x1(g, i)
                    if i == E + 5:
                        add_out(h, 0)
                    if i == E + 7 and g is not None:
                        low_z(g, 0)
                if g is not None:
                    low_z(g, 1)
                add_out(h, 1)

            def iteration(g, first=False, last=False):
                if not first:
                    before_exp, after_exp = route(g - 1)
                for b in range(GB):
                    dve.wait_ge(x0t_hi, GB * g + b + 1)
                    low(GT[:, b, 0, 1, :], bank[b][:, :], GT[:, b, 0, 0, :]).then_inc(x0t_lo, 1)
                for k in range(2 * GB):
                    if k == 3 and not first:
                        before_exp()
                    dve.wait_ge(gt_hi, 2 * GB * g + k + 1)
                    low(GT[:, k // 2, 1 + k % 2, 1, :], bank[GT_BANK[k]][:, :],
                        GT[:, k // 2, 1 + k % 2, 0, :]).then_inc(gt_lo, 1)
                if not first:
                    after_exp()

                def low_y2(p):
                    dve.wait_ge(y2_hi, 2 * g + p + 1)
                    low(y2s[:, 1, 2 * p:2 * p + 2], Q[:, 2, 2 * p:2 * p + 2],
                        y2s[:, 0, 2 * p:2 * p + 2]).then_inc(y2_lo, 1)

                if first:
                    dve.wait_ge(wsp_lo, 2)
                for i in range(T):
                    dve.wait_ge(q_mm, T * g + i + 1)
                    src = bank[GT_BANK[i % 4]][:, 0:BABY * D].rearrange("p (j c) -> p j c", c=D)
                    v.tensor_tensor(Q[:, :, i % NT, i // NT, :], src, bias[:, i % NT], ALU.add).then_inc(q_ready, 1)
                    if i == T - 2:
                        low_y2(0)
                low_y2(1)

                def low_y1(p):
                    dve.wait_ge(y1_hi, 2 * g + p + 1)
                    low(y1s[:, 1, 2 * p:2 * p + 2], y1[:, 2 * p:2 * p + 2],
                        y1s[:, 0, 2 * p:2 * p + 2]).then_inc(y1_lo, 1)

                for t in range(NT):
                    dve.wait_ge(y1_mm, NT * g + t + 1)
                    if t == 0:
                        dve.wait_ge(y2_lo, 2 * g + 2)
                    v.tensor_tensor(y1[:, t], bank[Y1_BANK[t]][:, 0:W].rearrange("p (b c) -> p b c", c=D),
                                    Q[:, 1, t], ALU.add).then_inc(y1_add, 1)
                    if t == 2:
                        low_y1(0)
                low_y1(1)
                if not last:
                    norm_x(g + 1)
                dve.wait_ge(xq_ready, g + 1)
                if not first:
                    dve.wait_ge(res_ready, g)
                for t in range(NT):
                    dve.wait_ge(h8_mm, NT * g + t + 1)
                    v.tensor_tensor(x1[:, t], bank[H8_BANK[t]][:, 0:W].rearrange("p (b c) -> p b c", c=D),
                                    Q[:, 0, t], ALU.add).then_inc(x1_add, 1)
                if first:
                    for part in range(10):
                        norm_x1(g, part)
                    for b in range(GB):
                        low_z(g, b)
                else:
                    experts(g - 1, g)

            iteration(0, first=True)
            with dve.Fori(1, GROUPS - 1) as g:
                iteration(g)
            iteration(GROUPS - 1, last=True)
            before_exp, after_exp = route(GROUPS - 1)
            before_exp()
            after_exp()
            experts(GROUPS - 1)

        @block.tensor
        def _(pe):
            def mm3(dst, wh, wl, xh, xl, start, stop):
                pe.matmul(dst, wh, xh, start=start, stop=False)
                pe.matmul(dst, wh, xl, start=False, stop=False)
                return pe.matmul(dst, wl, xh, start=False, stop=stop)

            pe.wait_ge(pool_const, 1)
            pe.wait_ge(rows_in, 80)
            R = NT + E + 2 + E
            pe.transpose(bank[0][:, 0:R], rows[:, :], ident[0:R, 0:R]).then_inc(rows_t, 1)
            pe.wait_ge(w_in, 32)
            pe.transpose(bank[1][:, 0:P], w_raw[:, 0, :], ident[:, :]).then_inc(w_t, 1)
            pe.wait_ge(wt_ready, 1)
            pe.matmul(bank[2][:, 0:P], wT[:, 1, :], wT[:, 0, :], start=True, stop=True).then_inc(weff_mm, 1)
            pe.wait_ge(lnat_ready, 1)
            for a in range(NT):
                for t in range(NT):
                    last = pe.transpose(bank[4 + a][:, t * P:(t + 1) * P], Lnat[:, t, a * P:(a + 1) * P], ident[:, :])
                last.then_inc(lt_mm, 1)

            pe.wait_ge(lnat_lo, 1)
            pe.wait_ge(lt_lo, NT)
            pe.wait_ge(pow_ready, 1)
            pe.matmul(bank[3][:, 0:P], RP[:, 1, :], RP[:, 1, :], start=True, stop=True).then_inc(pow_mm, 1)

            def power_tile(k, a):
                for t in range(NT):
                    c = slice(a * P, (a + 1) * P)
                    last = mm3(bank[4 + a][:, :], Lns[:, 0, t, c], Lns[:, 1, t, c],
                               LT[:, k - 1, 0, t, :], LT[:, k - 1, 1, t, :], t == 0, t == NT - 1)
                last.then_inc(lt_mm, 1)

            power_tile(1, 0)
            pe.wait_ge(pow_ready, 2)
            pe.matmul(bank[2][:, 0:2 * P], RP[:, 2, :], RP[:, 1:3, :], start=True, stop=True).then_inc(pow_mm, 1)
            power_tile(1, 1)
            pe.wait_ge(pow_ready, 3)
            pe.matmul(bank[3][:, :], RP[:, 4, :], RP[:, 1:5, :], start=True, stop=True).then_inc(pow_mm, 1)
            power_tile(1, 2)
            power_tile(1, 3)
            pe.wait_ge(pow_ready, 4)
            for c in range(BABY):
                pe.matmul(bank[c][:, 0:BABY * D], cols[:, FB_COL:FB_COL + 1].to_broadcast([P, P]),
                          RP[:, BABY * c:BABY * (c + 1), :], start=True, stop=True).then_inc(crep_mm, 1)
            pe.wait_ge(v1_ready, 1)
            for t in range(NT):
                for m in range(NT):
                    for s in range(2):
                        last = pe.matmul(bank[3][:, 2 * t:2 * t + 2], LT[:, 0, s, m, t * P:(t + 1) * P],
                                         ones_v[:, m, :], start=(m == 0 and s == 0), stop=(m == NT - 1 and s == 1))
            last.then_inc(v2_mm, 1)
            pe.wait_ge(lt_lo, 2 * NT)
            for a in range(NT):
                power_tile(2, a)
            for c in range(BABY):
                pe.wait_ge(crep_ready, c + 1)
                pe.matmul(bank[c][:, 0:BABY * D], w_raw[:, 1, :], RP[:, BABY * c:BABY * (c + 1), :],
                          start=True, stop=True).then_inc(fr_mm, 1)

            def transpose_x0(g, first):
                pe.wait_ge(x0_ready, g + 1)
                for b in range(GB):
                    if first:
                        pe.wait_ge(m_sum, b + 1)
                    for t in range(NT):
                        last = pe.transpose(bank[b][:, t * P:(t + 1) * P], x0[:, t, b, :], ident[:, :])
                    last.then_inc(x0t_mm, 1)

            def nodes_product(g, k):
                b, pw = k // 2, k % 2
                for t in range(NT):
                    wh, wl = x0s[:, 0, t, b, :], x0s[:, 1, t, b, :]
                    last = mm3(bank[GT_BANK[k]][:, :], wh, wl, LT[:, pw, 0, t, :], LT[:, pw, 1, t, :],
                               t == 0, t == NT - 1)
                last.then_inc(gt_mm, 1)

            def horner(src, banks, done, g, ready):
                for p in range(2):
                    pe.wait_ge(ready, 2 * g + p + 1)
                    for t in range(NT):
                        yield p, t
                        for m in (2 * p, 2 * p + 1):
                            c = slice(t * P, (t + 1) * P)
                            last = mm3(bank[banks[t]][:, 0:W], LT[:, 2, 0, m, c], LT[:, 2, 1, m, c],
                                       src[:, 0, m], src[:, 1, m], m == 0, m == NT - 1)
                        if p == 1:
                            last.then_inc(done, 1)

            def logits(h):
                pe.wait_ge(zt_lo, GB * h + GB)
                for t in range(T):
                    for s in range(2):
                        c = slice((t // GB) * P, (t // GB + 1) * P)
                        last = pe.matmul(bank[LG_BANK][:, t * C:(t + 1) * C], zT[:, s, t % GB, c], rts[:, :],
                                         start=(s == 0), stop=(s == 1))
                last.then_inc(lg_mm, 1)

            def transpose_comb(h):
                pe.wait_ge(comb_ready, h + 1)
                for b in range(GB):
                    for t in range(NT):
                        last = pe.transpose(bank[CT_BANK[b]][0:C, t * P:(t + 1) * P], cc[:, t * GB + b, :], ident[:, :])
                    last.then_inc(ct_mm, 1)

            def transpose_z(g, b, h=None):
                pe.wait_ge(z_ready, g + 1)
                if b == 1 and h is not None:
                    pe.wait_ge(out_add, 1 + GB * h + 1)
                for t in range(NT):
                    last = pe.transpose(bank[ZT_BANK[b]][:, t * P:(t + 1) * P], z[:, t, b, :], ident[:, :])
                last.then_inc(zt_mm, 1)

            def transpose_out(h, b, g=None):
                pe.wait_ge(yt_copied, GB * h + b + 1)
                if b == 1 and g is not None:
                    pe.wait_ge(zt_lo, GB * g + 1)
                for t in range(NT):
                    last = pe.transpose(bank[OT_BANK[b]][:, t * P:(t + 1) * P], yT[:, t * P:(t + 1) * P], ident[:, :])
                last.then_inc(ot_mm, 1)

            def experts(h, g=None):
                for s in range(ITEMS + LAG):
                    if s < ITEMS:
                        b, e = s // E, s % E
                        if s >= 2:
                            pe.wait_ge(gelu_done, ITEMS * h + s - 1)
                        elif g is not None:
                            pe.wait_ge(x1_add, NT * g + s + 1)
                        mm3(bank[UP_BANK[s % 2]][:, :], w1s[:, 0, e, :], w1s[:, 1, e, :],
                            zT[:, 0, b, :], zT[:, 1, b, :], True, True).then_inc(up_mm, 1)
                        if s >= 2:
                            pe.wait_ge(sc_ready, ITEMS * h + s - 1)
                        elif g is not None:
                            pe.wait_ge(x1_add, NT * g + s + 3)
                        pe.matmul(bank[REP_BANK[s % 2]][:, :], sel[:, e, :], combT[:, b, :],
                                  start=True, stop=True).then_inc(rep_mm, 1)
                    if s == ITEMS - 1 and g is not None:
                        transpose_z(g, 1, h)
                    i = s - LAG
                    if i >= 0:
                        b, e = i // E, i % E
                        dst = bank[SUM_BANK[b]][:, :]
                        if e == 0:
                            for k in range(2):
                                pe.matmul(dst, b2s[:, k, :], combT[:, b, :], start=(k == 0), stop=False)
                        pe.wait_ge(sc_lo, ITEMS * h + i + 1)
                        mm3(dst, w2s[:, 0, e, :], w2s[:, 1, e, :], scs[:, i % RING, 0, :], scs[:, i % RING, 1, :],
                            False, e == E - 1).then_inc(down_mm, 1)
                    if s == E + LAG + 1:
                        transpose_out(h, 0)
                    if s == E + LAG + 2 and g is not None:
                        transpose_z(g, 0)
                transpose_out(h, 1, g)

            def iteration(g, first=False):
                transpose_x0(g, first)
                pe.wait_ge(x0_lo, g + 1)
                for k in range(2 * GB):
                    if k == 0 and first:
                        pe.wait_ge(m_sum, BABY)
                    if k == 1 and first:
                        pe.wait_ge(v2_read, 1)
                    if k == 0 and not first:
                        pe.wait_ge(zt_lo, GB * g)
                    if k == 1 and not first:
                        pe.wait_ge(out_add, 1 + GB * (g - 1))
                    if k >= 2:
                        pe.wait_ge(x0t_lo, GB * g + k - 1)
                    nodes_product(g, k)
                    if k == 1 and not first:
                        logits(g - 1)
                if first:
                    pe.wait_ge(m_lo, 1)
                for i in range(T):
                    b, t = i // NT, i % NT
                    pe.wait_ge(gt_lo, 2 * GB * g + max(2 * b + 2, min(i + 1, 2 * GB)))
                    if i >= 4:
                        pe.wait_ge(q_ready, T * g + i - 3)
                    dst = bank[GT_BANK[i % 4]][:, 0:BABY * D]
                    c = slice(t * P, (t + 1) * P)
                    for k in range(BABY):
                        last = mm3(dst, GT[:, b, k, 0, c], GT[:, b, k, 1, c], M[:, 0, :, k, :], M[:, 1, :, k, :],
                                   k == 0, k == BABY - 1)
                    last.then_inc(q_mm, 1)
                if first:
                    pe.wait_ge(lt_lo, BABY * NT)
                else:
                    transpose_comb(g - 1)
                for p, t in horner(y2s, Y1_BANK, y1_mm, g, y2_lo):
                    if p == 0 and t >= 2:
                        pe.wait_ge(q_ready, T * g + NT + t + 1)
                if not first:
                    pe.wait_ge(ct_copied, GB * g)
                for _ in horner(y1s, H8_BANK, h8_mm, g, y1_lo):
                    pass
                if first:
                    for b in range(GB):
                        transpose_z(g, b)
                else:
                    experts(g - 1, g)

            iteration(0, first=True)
            with pe.Fori(1, GROUPS - 1) as g:
                iteration(g)
            iteration(GROUPS - 1)
            logits(GROUPS - 1)
            transpose_comb(GROUPS - 1)
            pe.wait_ge(small_ready, 2)
            pe.wait_ge(ct_copied, GB * GROUPS)
            experts(GROUPS - 1)


_INS = ['x', 'adj', 'L0_gnn_alpha_train', 'L0_gnn_w', 'L0_gnn_d', 'L0_gnn_fc_in_w', 'L0_gnn_fc_in_b',
        'L0_ffn_router_w', 'L0_ffn_w1', 'L0_ffn_b1', 'L0_ffn_w2', 'L0_ffn_b2']


def kernel(**inputs):
    import numpy as _np
    import concourse.bacc as _bacc
    from concourse import mybir as _mybir
    from concourse.bass_utils import run_bass_kernel_spmd as _run

    nc = _bacc.Bacc("TRN2", target_bir_lowering=False, num_devices=1)
    arrays, args = {}, []
    for name in _INS:
        a = _np.ascontiguousarray(inputs[name])
        arrays[f"in_{name}_dram"] = a
        args.append(nc.dram_tensor(f"in_{name}_dram", a.shape, _mybir.dt.from_np(a.dtype), kind="ExternalInput").ap())
    shape = arrays["in_x_dram"].shape
    args.append(nc.dram_tensor("out_0_dram", shape, _mybir.dt.float32, kind="ExternalOutput").ap())
    build(nc, *args)
    r = _run(nc, [arrays], core_ids=[0])
    return r.results[0]["out_0_dram"]
```

```python
import concourse.bass as bass
from concourse import mybir
from contextlib import ExitStack
from math import comb as binomial

FP32 = mybir.dt.float32
F32R = mybir.dt.float32r
I32 = mybir.dt.int32
ALU = mybir.AluOpType
ACT = mybir.ActivationFunctionType
AX = mybir.AxisListType

P = 128
STEPS = 8
DT = 1.0 / STEPS
EPS = 1e-5
BABY = 3
LAG = 4
RING = 5


def build(nc, x, adj, alpha, w, d, fc_w, fc_b, router_w, w1, b1, w2, b2, out):
    B, N, D = x.shape
    E = router_w.shape[0]
    NT = N // P
    GB = 2
    GROUPS = B // GB
    T = NT * GB
    ITEMS = GB * E
    W = GB * D
    C = 2 * E
    K = STEPS + 1
    assert D == P and K == BABY * BABY and N == 512

    ctx = ExitStack()
    with ctx:
        def sb(name, shape, dt=FP32):
            return ctx.enter_context(nc.sbuf_tensor(name, shape, dt))

        def sem(name):
            return ctx.enter_context(nc.semaphore(name))

        ident = sb("ident", [P, P])
        ident_dt = sb("ident_dt", [P, P])
        rows = sb("rows", [NT + E + 2 + E, P])
        cols = sb("cols", [P, NT + E + 2 + E])
        A_COL, B1_COL, D_COL, FB_COL, RT_COL = 0, NT, NT + E, NT + E + 1, NT + E + 2
        node = sb("node", [P, 6, NT])
        ones_v = sb("ones_v", [P, NT, 2], F32R)
        dclip = sb("dclip", [P, 1])
        w_raw = sb("w_raw", [P, 2, P])
        wT = sb("wT", [P, 2, P])
        LT = sb("LT", [P, BABY, 2, NT, N], F32R)
        M = sb("M", [P, 2, BABY, BABY, D], F32R)
        bias = sb("bias", [P, NT, BABY, D])
        w1s = sb("w1s", [P, 2, E, D], F32R)
        w2s = sb("w2s", [P, 2, E, D], F32R)
        b2s = sb("b2s", [C, 2, D], F32R)
        rts = sb("rts", [P, C], F32R)
        sel = sb("sel", [C, E, P], F32R)
        rank_i = sb("rank_i", [P, T, E], I32)
        rank = sb("rank", [P, T, E])
        nhalf = sb("nhalf", [P, T])

        xn = sb("xn", [P, NT, GB, D])
        xg = sb("xg", [P, NT, GB, D])
        x0 = sb("x0", [P, NT, GB, D])
        x0s = sb("x0s", [P, 2, NT, GB, D], F32R)
        GT = sb("GT", [P, GB, BABY, 2, N], F32R)
        y2s = GT[:, 0, :, :, :].rearrange("p i s n -> p (i s n)")[:, 0:2 * T * D] \
            .rearrange("p (s t b c) -> p s t b c", s=2, t=NT, b=GB)
        y1s = GT[:, 1, :, :, :].rearrange("p i s n -> p (i s n)")[:, 0:2 * T * D] \
            .rearrange("p (s t b c) -> p s t b c", s=2, t=NT, b=GB)
        Q = sb("Q", [P, BABY, NT, GB, D])
        y1 = Q[:, 2]
        x1 = Q[:, 0]
        w12_raw = Q[:, 0:2].rearrange("p k t b c -> p k (t b) c")
        Rp = Q[:, 2].rearrange("p t b c -> p (t b) c")
        scr = sb("scr", [P, 2, K, D])
        SK = scr[:, 0]
        crep = scr[:, 1]
        z = scr[:, 0, 0:T, :].rearrange("p (t b) c -> p t b c", b=GB)
        res = scr[:, 1, 0:T, :].rearrange("p (t b) c -> p t b c", b=GB)
        bn = sb("bn", [P, 2, T, 6])
        mv = sb("mv", [P, 2, 3, T])
        ve = sb("ve", [P, 2, T])
        rstd = sb("rstd", [P, 2, T])
        zT = sb("zT", [P, 2, GB, N], F32R)
        rt = sb("rt", [P, 6, T, E])
        rm = sb("rm", [P, 10, T])
        cc = sb("cc", [P, T, C])
        combT = sb("combT", [C, GB, N], F32R)
        work = sb("work", [P, 5, N])
        hid = work[:, 0:2]
        scaled = work[:, 2:5]
        Lnat = work[:, 0:4]
        scs = sb("scs", [P, RING, 2, N], F32R)
        Lns = scs[:, 0:NT, :, :].rearrange("p r s n -> p s r n")
        yT = sb("yT", [P, N])
        outs = sb("outs", [P, GB, NT, D])
        b2_raw = yT[0:C, 0:D]
        sel_raw = outs[0:C, :, :, :].rearrange("p b t c -> p (b t) c")

        bank = [ctx.enter_context(nc.psum_tensor(f"bank{i}", [P, 512], FP32)) for i in range(8)]

        rows_in, alpha_in, w_in, fc_in, w12_in, b2_in = (
            sem(n) for n in ("rows_in", "alpha_in", "w_in", "fc_in", "w12_in", "b2_in"))
        adj_in = [sem(f"adj_in{t}") for t in range(NT)]
        adj_scaled = sem("adj_scaled")
        pool_const, pool_own = sem("pool_const"), sem("pool_own")
        rows_t, w_t, cols_ready, sig_exp = sem("rows_t"), sem("w_t"), sem("cols_ready"), sem("sig_exp")
        node_ready = sem("node_ready")
        set_own = sem("set_own")
        lnat_ready, lnat_hi, lnat_lo = sem("lnat_ready"), sem("lnat_hi"), sem("lnat_lo")
        wt_ready, weff_mm = sem("wt_ready"), sem("weff_mm")
        pow_mm, pow_ready = sem("pow_mm"), sem("pow_ready")
        lt_mm, lt_hi, lt_lo = sem("lt_mm"), sem("lt_hi"), sem("lt_lo")
        fr_mm, crep_mm, crep_ready = sem("fr_mm"), sem("crep_mm"), sem("crep_ready")
        m_sum, m_hi, m_lo = sem("m_sum"), sem("m_hi"), sem("m_lo")
        v1_ready, v2_mm, v2_read = sem("v1_ready"), sem("v2_mm"), sem("v2_read")
        wsp_hi, wsp_lo = sem("wsp_hi"), sem("wsp_lo")
        small_ready = sem("small_ready")

        x_in = sem("x_in")
        xg_copied = sem("xg_copied")
        ln_own = [sem("ln1_own"), sem("ln2_own")]
        ln_ve = [sem("ln1_ve"), sem("ln2_ve")]
        ln_rstd = [sem("ln1_rstd"), sem("ln2_rstd")]
        x0_ready, x0_hi, x0_lo = sem("x0_ready"), sem("x0_hi"), sem("x0_lo")
        x0t_mm, x0t_hi, x0t_lo = sem("x0t_mm"), sem("x0t_hi"), sem("x0t_lo")
        gt_mm, gt_hi, gt_lo = sem("gt_mm"), sem("gt_hi"), sem("gt_lo")
        q_mm, q_ready = sem("q_mm"), sem("q_ready")
        y2_hi, y2_lo = sem("y2_hi"), sem("y2_lo")
        y1_mm, y1_add = sem("y1_mm"), sem("y1_add")
        y1_hi, y1_lo = sem("y1_hi"), sem("y1_lo")
        xq_ready = sem("xq_ready")
        h8_mm, x1_add = sem("h8_mm"), sem("x1_add")
        z_ready, res_ready = sem("z_ready"), sem("res_ready")
        zt_mm, zt_hi, zt_lo = sem("zt_mm"), sem("zt_hi"), sem("zt_lo")
        lg_mm, rt_own, rt_pre, rt_exp, comb_ready = (sem(n) for n in ("lg_mm", "rt_own", "rt_pre", "rt_exp", "comb_ready"))
        ct_mm, ct_copied = sem("ct_mm"), sem("ct_copied")
        up_mm, gelu_done, rep_mm, sc_ready = sem("up_mm"), sem("gelu_done"), sem("rep_mm"), sem("sc_ready")
        sc_hi, sc_lo, down_mm = sem("sc_hi"), sem("sc_lo"), sem("down_mm")
        yt_copied, ot_mm = sem("yt_copied"), sem("ot_mm")
        out_add = sem("out_add")
        out_stored = sem("out_stored")
        LN_OWN = T + 2
        RT_OWN = 23

        GT_BANK = [2, 3, 0, 1]
        Y1_BANK = [2, 3, 0, 1]
        H8_BANK = [4, 5, 6, 7]
        UP_BANK, REP_BANK, SUM_BANK = [4, 5], [6, 7], [0, 1]
        X0_BANK = [0, 4]
        CREP_BANK, FR_BANK = [1, 2, 3], [2, 0, 7]
        ZT_BANK, OT_BANK, LG_BANK, CT_BANK = [3, 2], [2, 3], 4, [5, 6]

        x_v = x.rearrange("(g b) (t p) c -> g b p t c", b=GB, p=P)
        out_v = out.rearrange("(g b) (t p) c -> g b p t c", b=GB, p=P)

        def of_group(v, g, b):
            return v[bass.ds(g, 1), b, :, :, :].rearrange("o p t c -> p (o t) c")

        block = ctx.enter_context(nc.Block())

        @block.sync
        def _(sp):
            sp.sem_inc(out_add, 1)
            sp.sem_inc(out_stored, 1)
            sp.dma_start(rows[A_COL:A_COL + NT, :], alpha.rearrange("(t p) -> t p", p=P)).then_inc(alpha_in, 16)
            for t in range(NT):
                sp.dma_start(Lnat[:, t, :], adj[t * P:(t + 1) * P, :]).then_inc(adj_in[t], 16)

            def load_x(g):
                for b in range(GB):
                    sp.dma_start(xn[:, :, b, :], of_group(x_v, g, b)).then_inc(x_in, 16)

            def next_x(g):
                sp.wait_ge(x0_ready, g)
                sp.wait_ge(xg_copied, g)
                load_x(g)

            def store(h):
                for b in range(GB):
                    sp.wait_ge(out_add, 1 + GB * h + b + 1)
                    sp.dma_start(of_group(out_v, h, b), outs[:, b, :, :]).then_inc(out_stored, 16)

            load_x(0)
            sp.dma_start(w_raw[:, 1, :], fc_w).then_inc(fc_in, 16)
            sp.dma_start(w12_raw[:, 0], w1.rearrange("e c f -> c e f")).then_inc(w12_in, 16)
            sp.dma_start(w12_raw[:, 1], w2.rearrange("e f c -> f e c")).then_inc(w12_in, 16)
            for r in (0, E):
                sp.dma_start(b2_raw[r:r + E, :], b2).then_inc(b2_in, 16)
            next_x(1)
            next_x(2)
            with sp.Fori(1, GROUPS - 2) as g:
                store(g - 1)
                next_x(g + 2)
            for h in range(GROUPS - 3, GROUPS):
                store(h)
            sp.wait_ge(out_stored, 1 + 32 * GROUPS)

        @block.gpsimd
        def _(pool):
            nc.gpsimd.memset(ident[:, :], 0.0).then_inc(pool_own, 1)
            pool.wait_ge(pool_own, 1)
            nc.gpsimd.affine_select(out=ident[:, :], in_=ident[:, :], compare_op=ALU.not_equal, fill=1.0,
                                    base=0, pattern=[[-1, P]], channel_multiplier=1).then_inc(pool_const, 1)
            nc.gpsimd.memset(sel_raw, 0.0).then_inc(pool_own, 1)
            for r in range(2):
                pool.wait_ge(pool_own, 2 + r)
                nc.gpsimd.affine_select(out=sel_raw, in_=sel_raw, compare_op=ALU.not_equal,
                                        fill=1.0, base=-r * E, pattern=[[-1, E], [0, P]],
                                        channel_multiplier=1).then_inc(pool_own, 1)
            nc.gpsimd.iota(rank_i[:, :, :], pattern=[[0, T], [-1, E]], base=E, channel_multiplier=0)
            nc.gpsimd.memset(nhalf[:, :], -0.5).then_inc(pool_own, 1)
            pool.wait_ge(pool_own, 5)
            nc.gpsimd.tensor_copy(rank[:, :, :], rank_i[:, :, :]).then_inc(pool_const, 1)

            def inverse_root(n, g):
                pool.wait_ge(ln_ve[n], g + 1)
                nc.gpsimd.tensor_tensor(rstd[:, n, :], ve[:, n, :], nhalf[:, :], ALU.pow).then_inc(ln_rstd[n], 1)

            def low_x0(g):
                pool.wait_ge(x0_hi, g + 1)
                nc.gpsimd.tensor_tensor(x0s[:, 1], x0[:, :, :, :], x0s[:, 0].bitcast(FP32),
                                        ALU.subtract).then_inc(x0_lo, 1)

            def item_low(h, i):
                pool.wait_ge(sc_hi, ITEMS * h + i + 1)
                nc.gpsimd.tensor_tensor(scs[:, i % RING, 1, :], scaled[:, i % 3, :],
                                        scs[:, i % RING, 0, :].bitcast(FP32), ALU.subtract).then_inc(sc_lo, 1)

            def residual(h):
                pool.wait_ge(z_ready, h + 1)
                pool.wait_ge(out_add, 1 + GB * h)
                nc.gpsimd.tensor_tensor(res, x1, z, ALU.add).then_inc(res_ready, 1)

            inverse_root(0, 0)
            low_x0(0)
            pool.wait_ge(lnat_hi, 1)
            nc.gpsimd.tensor_tensor(Lns[:, 1], Lnat, Lns[:, 0].bitcast(FP32), ALU.subtract).then_inc(lnat_lo, 1)
            for k in range(2):
                pool.wait_ge(wsp_hi, k + 1)
                nc.gpsimd.tensor_tensor((w1s, w2s)[k][:, 1], w12_raw[:, k],
                                        (w1s, w2s)[k][:, 0].bitcast(FP32), ALU.subtract).then_inc(wsp_lo, 1)

            def iteration(g, first=False, final=False):
                if not first:
                    residual(g - 1)
                if not final:
                    inverse_root(0, g + 1)
                pool.wait_ge(xg_copied, g + 1)
                pool.wait_ge(q_ready, T * g + T)
                nc.gpsimd.tensor_tensor(Q[:, 0], Q[:, 0], xg[:, :, :, :], ALU.add).then_inc(xq_ready, 1)
                if not final:
                    low_x0(g + 1)
                if first:
                    inverse_root(1, g)
                else:
                    for i in range(ITEMS):
                        item_low(g - 1, i)
                        if i == 3:
                            inverse_root(1, g)

            iteration(0, first=True)
            with pool.Fori(1, GROUPS - 1) as g:
                iteration(g)
            iteration(GROUPS - 1, final=True)
            residual(GROUPS - 1)
            for i in range(ITEMS):
                item_low(GROUPS - 1, i)

        @block.scalar
        def _(act):
            for k, src in ((D_COL, d), (FB_COL, fc_b)):
                act.dma_start(rows[k:k + 1, :], src.rearrange("(o p) -> o p", o=1)).then_inc(rows_in, 16)
            act.dma_start(w_raw[:, 0, :], w).then_inc(w_in, 16)
            for k, src in ((B1_COL, b1), (RT_COL, router_w)):
                act.dma_start(rows[k:k + E, :], src).then_inc(rows_in, 16)

            def high(dst, src):
                return nc.scalar.activation(dst, src, ACT.Copy)

            act.wait_ge(cols_ready, 1)
            nc.scalar.activation(node[:, 0, :], cols[:, A_COL:A_COL + NT], ACT.Exp, scale=-1.0).then_inc(sig_exp, 1)

            def high_x0(g):
                act.wait_ge(x0_ready, g + 1)
                high(x0s[:, 0], x0[:, :, :, :]).then_inc(x0_hi, 1)

            def copy_x(g):
                if isinstance(g, int) and g == 0:
                    act.wait_ge(x_in, 32)
                else:
                    act.wait_ge(x0_ready, g + 1)
                    act.wait_ge(xq_ready, g)
                high(xg[:, :, :, :], xn[:, :, :, :]).then_inc(xg_copied, 1)

            def high_x0t(g):
                for b in range(GB):
                    act.wait_ge(x0t_mm, GB * g + b + 1)
                    high(GT[:, b, 0, 0, :], bank[X0_BANK[b]][:, :]).then_inc(x0t_hi, 1)

            def high_gt(g, k, turn):
                act.wait_ge(gt_mm, 2 * GB * g + turn + 1)
                high(GT[:, k // 2, 1 + k % 2, 0, :], bank[GT_BANK[k]][:, :]).then_inc(gt_hi, 1)

            def high_lt(k):
                for a in range(NT):
                    act.wait_ge(lt_mm, NT * k + a + 1)
                    high(LT[:, k, 0, a, :], bank[4 + a][:, :]).then_inc(lt_hi, 1)

            act.wait_ge(node_ready, 1)
            for t in range(NT):
                act.wait_ge(adj_in[t], 16)
                nc.scalar.activation(Lnat[:, t, :], Lnat[:, t, :], ACT.Copy,
                                     scale=node[:, 3, t:t + 1]).then_inc(adj_scaled, 1)
            act.wait_ge(lnat_ready, NT)
            high(Lns[:, 0], Lnat).then_inc(lnat_hi, 1)
            high_lt(0)
            high_x0(0)
            copy_x(0)
            high_x0t(0)
            high_gt(0, 0, 0)
            high_gt(0, 2, 1)
            high_lt(1)
            act.wait_ge(w12_in, 32)
            high(w1s[:, 0], w12_raw[:, 0]).then_inc(wsp_hi, 1)
            high(w2s[:, 0], w12_raw[:, 1]).then_inc(wsp_hi, 1)
            act.wait_ge(pool_own, 5)
            high(sel[:, :, :], sel_raw).then_inc(small_ready, 1)
            high_gt(0, 1, 2)
            high_gt(0, 3, 3)
            act.wait_ge(m_sum, BABY)
            high(M[:, 0], SK.rearrange("p (j i) c -> p j i c", i=BABY)).then_inc(m_hi, 1)
            high_lt(2)

            def copy_sum(h, b):
                act.wait_ge(down_mm, ITEMS * h + E * (b + 1))
                if b:
                    act.wait_ge(ot_mm, GB * h + b)
                high(yT[:, :], bank[SUM_BANK[b]][:, :]).then_inc(yt_copied, 1)

            def high_z(g, b):
                act.wait_ge(zt_mm, GB * g + b + 1)
                high(zT[:, 0, b, :], bank[ZT_BANK[b]][:, :]).then_inc(zt_hi, 1)

            def route_exp(h):
                act.wait_ge(rt_pre, h + 1)
                nc.scalar.activation(rt[:, 1], rt[:, 0], ACT.Exp).then_inc(rt_exp, 1)

            def copy_comb(h):
                for b in range(GB):
                    act.wait_ge(ct_mm, GB * h + b + 1)
                    high(combT[:, b, :], bank[CT_BANK[b]][0:C, :]).then_inc(ct_copied, 1)

            def item_high(h, i):
                act.wait_ge(sc_ready, ITEMS * h + i + 1)
                if i >= RING:
                    act.wait_ge(down_mm, ITEMS * h + i - RING + 1)
                high(scs[:, i % RING, 0, :], scaled[:, i % 3, :]).then_inc(sc_hi, 1)

            def experts(h, g=None, more=False):
                for i in range(ITEMS):
                    act.wait_ge(up_mm, ITEMS * h + i + 1)
                    if i >= 2:
                        act.wait_ge(sc_ready, ITEMS * h + i - 1)
                    e = i % E
                    nc.scalar.activation(hid[:, i % 2, :], bank[UP_BANK[i % 2]][:, :], ACT.Gelu,
                                         bias=cols[:, B1_COL + e:B1_COL + e + 1]).then_inc(gelu_done, 1)
                    if i >= 1:
                        item_high(h, i - 1)
                    if i == E + LAG:
                        copy_sum(h, 0)
                    if i == E + 6 and g is not None:
                        high_z(g, 0)
                if g is not None:
                    high_z(g, 1)
                item_high(h, ITEMS - 1)
                if more:
                    high_x0t(g + 1)
                copy_sum(h, 1)

            def iteration(g, first=False, final=False):
                if not first:
                    high_gt(g, 2, 2)
                    route_exp(g - 1)
                    high_gt(g, 3, 3)
                for p in range(2):
                    act.wait_ge(q_ready, T * g + NT + 2 * p + 2)
                    high(y2s[:, 0, 2 * p:2 * p + 2], Q[:, 2, 2 * p:2 * p + 2]).then_inc(y2_hi, 1)
                if not first:
                    copy_comb(g - 1)
                if not final:
                    high_x0(g + 1)
                for t in range(NT):
                    act.wait_ge(y1_add, NT * g + t + 1)
                    high(y1s[:, 0, t], y1[:, t]).then_inc(y1_hi, 1)
                if not final:
                    copy_x(g + 1)
                if first:
                    high_x0t(g + 1)
                    for k in range(2):
                        high_gt(g + 1, k, k)
                    for b in range(GB):
                        high_z(g, b)
                else:
                    experts(g - 1, g, not final)
                    if not final:
                        for k in range(2):
                            high_gt(g + 1, k, k)

            iteration(0, first=True)
            with act.Fori(1, GROUPS - 1) as g:
                iteration(g)
            iteration(GROUPS - 1, final=True)
            route_exp(GROUPS - 1)
            copy_comb(GROUPS - 1)
            experts(GROUPS - 1)

        @block.vector
        def _(dve):
            v = nc.vector

            def low(dst, src, hi):
                return v.tensor_tensor(dst, src, hi.bitcast(FP32), ALU.subtract)

            def ln_stats(n, g, src, t):
                v.bn_stats(bn[:, n, t, :], src[:, t // GB, t % GB, :]).then_inc(ln_own[n], 1)

            def ln_var(n, g):
                mean_e, mean_o = bn[:, n, :, 1], bn[:, n, :, 4]
                dve.wait_ge(ln_own[n], LN_OWN * g + T)
                v.tensor_tensor(mv[:, n, 1, :], mean_e, mean_o, ALU.subtract)
                v.tensor_tensor(mv[:, n, 2, :], bn[:, n, :, 2], bn[:, n, :, 5], ALU.add)
                v.tensor_tensor(mv[:, n, 0, :], mean_e, mean_o, ALU.add).then_inc(ln_own[n], 1)
                dve.wait_ge(ln_own[n], LN_OWN * g + T + 1)
                v.tensor_tensor(mv[:, n, 1, :], mv[:, n, 1, :], mv[:, n, 1, :], ALU.mult)
                v.tensor_scalar(mv[:, n, 0, :], mv[:, n, 0, :], 0.5, None, ALU.mult)
                v.tensor_scalar(mv[:, n, 2, :], mv[:, n, 2, :], 1.0 / D, EPS, ALU.mult, ALU.add).then_inc(ln_own[n], 1)
                dve.wait_ge(ln_own[n], LN_OWN * g + T + 2)
                v.scalar_tensor_tensor(out=ve[:, n, :], in0=mv[:, n, 1, :], scalar=0.25, in1=mv[:, n, 2, :],
                                       op0=ALU.mult, op1=ALU.add).then_inc(ln_ve[n], 1)

            def ln_scale(n, dst, src, t):
                return v.tensor_scalar(dst[:, t // GB, t % GB, :], src[:, t // GB, t % GB, :],
                                       mv[:, n, 0, t:t + 1], rstd[:, n, t:t + 1], ALU.subtract, ALU.mult)

            def norm_x_stats(g, tiles):
                for t in tiles:
                    if t == 0:
                        dve.wait_ge(x_in, 32 * g + 32)
                    ln_stats(0, g, xn, t)

            def norm_x_scale(g):
                dve.wait_ge(ln_rstd[0], g + 1)
                for t in range(T):
                    last = ln_scale(0, x0, xn, t)
                last.then_inc(x0_ready, 1)

            own = [0]

            def step(ins):
                own[0] += 1
                ins.then_inc(set_own, 1)
                dve.wait_ge(set_own, own[0])

            def low_lt(k):
                for a in range(NT):
                    dve.wait_ge(lt_hi, NT * k + a + 1)
                    low(LT[:, k, 1, a, :], bank[4 + a][:, :], LT[:, k, 0, a, :]).then_inc(lt_lo, 1)

            def low_x0t(g, b):
                dve.wait_ge(x0t_hi, GB * g + b + 1)
                low(GT[:, b, 0, 1, :], bank[X0_BANK[b]][:, :], GT[:, b, 0, 0, :]).then_inc(x0t_lo, 1)

            def low_gt(g, k, turn):
                dve.wait_ge(gt_hi, 2 * GB * g + turn + 1)
                low(GT[:, k // 2, 1 + k % 2, 1, :], bank[GT_BANK[k]][:, :],
                    GT[:, k // 2, 1 + k % 2, 0, :]).then_inc(gt_lo, 1)

            def power_out(n, first, count, src):
                dve.wait_ge(pow_mm, n)
                v.tensor_copy(Rp[:, first - 1:first - 1 + count, :],
                              src[:, 0:count * P].rearrange("p (k c) -> p k c", c=P)).then_inc(pow_ready, 1)

            dve.wait_ge(rows_t, 1)
            v.tensor_copy(cols[:, :], bank[0][:, 0:NT + E + 2 + E]).then_inc(cols_ready, 1)
            dve.wait_ge(cols_ready, 1)
            step(v.tensor_scalar(dclip[:, :], cols[:, D_COL:D_COL + 1], 0.0, 1.0, ALU.max, ALU.min))
            dve.wait_ge(sig_exp, 1)
            step(v.tensor_scalar(node[:, 1, :], node[:, 0, :], 1.0, None, ALU.add))
            step(v.reciprocal(node[:, 2, :], node[:, 1, :]))
            v.tensor_scalar(node[:, 3, :], node[:, 2, :], DT * 0.5, None, ALU.mult).then_inc(node_ready, 1)
            step(v.tensor_scalar(node[:, 0, :], node[:, 2, :], -DT * 0.5, 1.0 - DT, ALU.mult, ALU.add))
            dve.wait_ge(w_t, 1)
            v.tensor_copy(wT[:, 0, :], bank[1][:, 0:P])
            v.tensor_scalar(wT[:, 1, :], bank[1][:, 0:P], dclip[:, :], None, ALU.mult).then_inc(wt_ready, 1)
            dve.wait_ge(pool_const, 1)
            v.tensor_scalar(ident_dt[:, :], ident[:, :], DT, None, ALU.mult)
            for t in range(NT):
                dve.wait_ge(adj_scaled, t + 1)
                diag = Lnat[:, t, t * P:(t + 1) * P]
                v.scalar_tensor_tensor(out=diag, in0=ident[:, :], scalar=node[:, 0, t:t + 1],
                                       in1=diag, op0=ALU.mult, op1=ALU.add).then_inc(lnat_ready, 1)
            dve.wait_ge(weff_mm, 1)
            v.tensor_scalar(Rp[:, 0, :], bank[2][:, 0:P], DT, None, ALU.mult).then_inc(pow_ready, 1)
            norm_x_stats(0, range(T))
            ln_var(0, 0)
            low_lt(0)
            power_out(1, 2, 1, bank[3])
            norm_x_scale(0)
            low_x0t(0, 0)
            low_x0t(0, 1)
            step(v.tensor_reduce(node[:, 4, :], Lnat, AX.X, ALU.add))
            step(v.tensor_copy(ones_v[:, :, 0], node[:, 4, :]))
            low(ones_v[:, :, 1], node[:, 4, :], ones_v[:, :, 0]).then_inc(v1_ready, 1)
            low_gt(0, 0, 0)
            power_out(2, 3, 2, bank[3])
            low_gt(0, 2, 1)
            power_out(3, 5, 4, bank[1])
            dve.wait_ge(pow_ready, 4)
            for i in range(1, STEPS):
                for k in range(STEPS - i):
                    last = v.scalar_tensor_tensor(out=SK[:, k, :], in0=Rp[:, i - 1, :], scalar=DT * binomial(k + i, i),
                                                  in1=ident_dt[:, :] if i == 1 else SK[:, k, :],
                                                  op0=ALU.mult, op1=ALU.add)
                step(last)
                if i == 3:
                    low_lt(1)
            step(v.tensor_copy(rts[:, 0:E], cols[:, RT_COL:RT_COL + E]))
            low(rts[:, E:C], cols[:, RT_COL:RT_COL + E], rts[:, 0:E])
            dve.wait_ge(b2_in, 32)
            step(v.tensor_copy(b2s[:, 0, :], b2_raw))
            low(b2s[:, 1, :], b2_raw, b2s[:, 0, :]).then_inc(small_ready, 1)
            for c in range(BABY):
                dve.wait_ge(crep_mm, c + 1)
                for r in range(BABY):
                    k = STEPS - (BABY * c + r)
                    last = v.tensor_scalar(crep[:, k, :], bank[CREP_BANK[c]][:, r * D:(r + 1) * D],
                                           float(binomial(STEPS, k)), None, ALU.mult)
                last.then_inc(crep_ready, 1)
            dve.wait_ge(v2_mm, 1)
            v.tensor_reduce(node[:, 5, :], bank[0][:, 0:2 * NT].rearrange("p (t s) -> p t s", s=2),
                            AX.X, ALU.add).then_inc(v2_read, 1)
            dve.wait_ge(v2_read, 1)
            dve.wait_ge(crep_ready, BABY)
            cj = crep.rearrange("p (j i) c -> p j i c", i=BABY)
            for i in (1, 2):
                for t in range(NT):
                    last = v.scalar_tensor_tensor(out=bias[:, t], in0=cj[:, :, i, :], scalar=node[:, 3 + i, t:t + 1],
                                                  in1=cj[:, :, 0, :] if i == 1 else bias[:, t],
                                                  op0=ALU.mult, op1=ALU.add)
                step(last)
            low_gt(0, 1, 2)
            low_gt(0, 3, 3)
            for c in range(BABY):
                dve.wait_ge(fr_mm, c + 1)
                for r in range(BABY):
                    k = STEPS - (BABY * c + r)
                    src = bank[FR_BANK[c]][:, r * D:(r + 1) * D]
                    if k == STEPS:
                        last = v.tensor_copy(SK[:, k, :], src)
                    else:
                        last = v.scalar_tensor_tensor(out=SK[:, k, :], in0=src, scalar=float(binomial(STEPS, k)),
                                                      in1=ident_dt[:, :] if k == STEPS - 1 else SK[:, k, :],
                                                      op0=ALU.mult, op1=ALU.add)
                last.then_inc(m_sum, 1)
            dve.wait_ge(m_hi, 1)
            low(M[:, 1], SK.rearrange("p (j i) c -> p j i c", i=BABY), M[:, 0]).then_inc(m_lo, 1)
            low_lt(2)

            def route(h):
                def per_token(k):
                    return rm[:, k, :].unsqueeze(2).to_broadcast([P, T, E])

                def largest(prob, k):
                    return [
                        lambda: v.tensor_reduce(rm[:, k, :], prob, AX.X, ALU.max),
                        lambda: v.tensor_tensor(rt[:, 5], prob, per_token(k), ALU.is_equal),
                        lambda: v.tensor_tensor(rt[:, 5], rt[:, 5], rank[:, :, :], ALU.mult),
                        lambda: v.tensor_reduce(rm[:, 9, :], rt[:, 5], AX.X, ALU.max),
                    ]

                lg = bank[LG_BANK][:, 0:T * C].rearrange("p (t s e) -> p t e s", s=2, e=E)
                before_exp = [
                    lambda: v.tensor_reduce(rt[:, 2], lg, AX.X, ALU.add),
                    lambda: v.tensor_reduce(rm[:, 0, :], rt[:, 2], AX.X, ALU.max),
                ]
                after_exp = [
                    lambda: v.tensor_reduce(rm[:, 1, :], rt[:, 1], AX.X, ALU.add),
                    lambda: v.reciprocal(rm[:, 2, :], rm[:, 1, :]),
                    lambda: v.tensor_tensor(rt[:, 0], rt[:, 1], per_token(2), ALU.mult),
                    *largest(rt[:, 0], 3),
                    lambda: v.tensor_tensor(rt[:, 3], rt[:, 5], per_token(9), ALU.is_equal),
                    lambda: v.scalar_tensor_tensor(out=rt[:, 2], in0=rt[:, 3], scalar=-2.0, in1=rt[:, 0],
                                                   op0=ALU.mult, op1=ALU.add),
                    *largest(rt[:, 2], 4),
                    lambda: v.tensor_tensor(rt[:, 4], rt[:, 5], per_token(9), ALU.is_equal),
                    lambda: v.tensor_tensor(rt[:, 3], rt[:, 3], rt[:, 4], ALU.add),
                    lambda: v.tensor_tensor(rm[:, 5, :], rm[:, 3, :], rm[:, 4, :], ALU.add),
                    lambda: v.tensor_scalar(rm[:, 6, :], rm[:, 5, :], 1e-12, None, ALU.max),
                    lambda: v.reciprocal(rm[:, 7, :], rm[:, 6, :]),
                    lambda: v.tensor_tensor(rt[:, 5], rt[:, 3], rt[:, 0], ALU.mult),
                    lambda: v.tensor_tensor(rt[:, 4], rt[:, 5], per_token(7), ALU.mult),
                    lambda: v.tensor_copy(cc[:, :, 0:E].bitcast(F32R), rt[:, 4]),
                ]
                assert len(before_exp) + len(after_exp) == RT_OWN, len(before_exp) + len(after_exp)

                def step(n):
                    (before_exp + after_exp)[n]().then_inc(rt_own, 1)
                    dve.wait_ge(rt_own, RT_OWN * h + n + 1)

                def start():
                    dve.wait_ge(lg_mm, h + 1)
                    for n in range(len(before_exp)):
                        step(n)
                    v.tensor_tensor(rt[:, 0], rt[:, 2], per_token(0), ALU.subtract).then_inc(rt_pre, 1)

                def go_on(part, parts):
                    if part == 0:
                        dve.wait_ge(rt_exp, h + 1)
                    n, m = len(before_exp), len(after_exp)
                    for k in range(n + m * part // parts, n + m * (part + 1) // parts):
                        step(k)
                    if part == parts - 1:
                        v.tensor_tensor(cc[:, :, E:C], rt[:, 4], cc[:, :, 0:E], ALU.subtract).then_inc(comb_ready, 1)

                return start, go_on

            def low_z(g, b):
                dve.wait_ge(zt_hi, GB * g + b + 1)
                low(zT[:, 1, b, :], bank[ZT_BANK[b]][:, :], zT[:, 0, b, :]).then_inc(zt_lo, 1)

            def add_out(h, b):
                dve.wait_ge(ot_mm, GB * h + b + 1)
                dve.wait_ge(res_ready, h + 1)
                dve.wait_ge(out_stored, 1 + 32 * h)
                v.tensor_tensor(outs[:, b, :, :], bank[OT_BANK[b]][:, :].rearrange("p (t c) -> p t c", c=D),
                                res[:, :, b, :], ALU.add).then_inc(out_add, 1)

            def scale_item(h, i):
                dve.wait_ge(gelu_done, ITEMS * h + i + 1)
                dve.wait_ge(rep_mm, ITEMS * h + i + 1)
                if i >= 3:
                    dve.wait_ge(sc_lo, ITEMS * h + i - 2)
                v.tensor_tensor(scaled[:, i % 3, :], hid[:, i % 2, :], bank[REP_BANK[i % 2]][:, :],
                                ALU.mult).then_inc(sc_ready, 1)

            def norm_x1(g, part):
                if part < 4:
                    if part == 0:
                        dve.wait_ge(x1_add, NT * g + NT)
                    for t in (2 * part, 2 * part + 1):
                        ln_stats(1, g, x1, t)
                elif part == 4:
                    ln_var(1, g)
                elif part < 10:
                    if part == 6:
                        dve.wait_ge(ln_rstd[1], g + 1)
                    if part >= 6:
                        for t in (2 * (part - 6), 2 * (part - 6) + 1):
                            last = ln_scale(1, z, x1, t)
                        if part == 9:
                            last.then_inc(z_ready, 1)

            def experts(h, g=None, more=False):
                for i in range(ITEMS):
                    scale_item(h, i)
                    if g is not None:
                        norm_x1(g, i)
                    if i == E + 5:
                        add_out(h, 0)
                    if i == E + 7 and g is not None:
                        low_z(g, 0)
                if g is not None:
                    low_z(g, 1)
                if more:
                    for b in range(GB):
                        low_x0t(g + 1, b)
                    low_gt(g + 1, 0, 0)
                add_out(h, 1)
                if more:
                    low_gt(g + 1, 1, 1)

            def iteration(g, first=False, final=False):
                if not first:
                    route_start, route_on = route(g - 1)
                    low_gt(g, 2, 2)
                if not final:
                    norm_x_stats(g + 1, range(T // 2))
                if not first:
                    route_start()
                    low_gt(g, 3, 3)
                if not final:
                    norm_x_stats(g + 1, range(T // 2, T))
                    ln_var(0, g + 1)

                def low_y2(p):
                    dve.wait_ge(y2_hi, 2 * g + p + 1)
                    low(y2s[:, 1, 2 * p:2 * p + 2], Q[:, 2, 2 * p:2 * p + 2],
                        y2s[:, 0, 2 * p:2 * p + 2]).then_inc(y2_lo, 1)

                if first:
                    dve.wait_ge(wsp_lo, 2)
                else:
                    dve.wait_ge(res_ready, g)
                for i in range(T):
                    dve.wait_ge(q_mm, T * g + i + 1)
                    src = bank[GT_BANK[i % 4]][:, 0:BABY * D].rearrange("p (j c) -> p j c", c=D)
                    v.tensor_tensor(Q[:, :, i % NT, i // NT, :], src, bias[:, i % NT], ALU.add).then_inc(q_ready, 1)
                    if not first and i < T - 1:
                        route_on(i, T - 1)
                    if i == T - 2:
                        low_y2(0)
                low_y2(1)
                if not final:
                    norm_x_scale(g + 1)

                def low_y1(t):
                    dve.wait_ge(y1_hi, NT * g + t + 1)
                    low(y1s[:, 1, t], y1[:, t], y1s[:, 0, t]).then_inc(y1_lo, 1)

                for t in range(NT):
                    dve.wait_ge(y1_mm, NT * g + t + 1)
                    if t == 0:
                        dve.wait_ge(y2_lo, 2 * g + 2)
                    v.tensor_tensor(y1[:, t], bank[Y1_BANK[t]][:, 0:W].rearrange("p (b c) -> p b c", c=D),
                                    Q[:, 1, t], ALU.add).then_inc(y1_add, 1)
                    if t >= 1:
                        low_y1(t - 1)
                low_y1(NT - 1)
                dve.wait_ge(xq_ready, g + 1)
                for t in range(NT):
                    dve.wait_ge(h8_mm, NT * g + t + 1)
                    v.tensor_tensor(x1[:, t], bank[H8_BANK[t]][:, 0:W].rearrange("p (b c) -> p b c", c=D),
                                    Q[:, 0, t], ALU.add).then_inc(x1_add, 1)
                if first:
                    for part in range(5):
                        norm_x1(g, part)
                    for b in range(GB):
                        low_x0t(g + 1, b)
                    for part in range(5, 10):
                        norm_x1(g, part)
                    for k in range(2):
                        low_gt(g + 1, k, k)
                    for b in range(GB):
                        low_z(g, b)
                else:
                    experts(g - 1, g, not final)

            iteration(0, first=True)
            with dve.Fori(1, GROUPS - 1) as g:
                iteration(g)
            iteration(GROUPS - 1, final=True)
            route_start, route_on = route(GROUPS - 1)
            route_start()
            route_on(0, 1)
            experts(GROUPS - 1)

        @block.tensor
        def _(pe):
            def mm3(dst, wh, wl, xh, xl, start, stop):
                pe.matmul(dst, wh, xh, start=start, stop=False)
                pe.matmul(dst, wh, xl, start=False, stop=False)
                return pe.matmul(dst, wl, xh, start=False, stop=stop)

            def nodes_product(g, k):
                b, pw = k // 2, k % 2
                for t in range(NT):
                    last = mm3(bank[GT_BANK[k]][:, :], x0s[:, 0, t, b, :], x0s[:, 1, t, b, :],
                               LT[:, pw, 0, t, :], LT[:, pw, 1, t, :], t == 0, t == NT - 1)
                last.then_inc(gt_mm, 1)

            def transpose_x0(g, b):
                for t in range(NT):
                    last = pe.transpose(bank[X0_BANK[b]][:, t * P:(t + 1) * P], x0[:, t, b, :], ident[:, :])
                last.then_inc(x0t_mm, 1)

            def times_powers(dst, left, c):
                first = BABY * c
                if first == 0:
                    pe.matmul(dst[:, 0:D], left, ident[:, :], start=True, stop=True)
                    first = 1
                return pe.matmul(dst[:, (first - BABY * c) * D:BABY * D], left, Rp[:, first - 1:BABY * (c + 1) - 1, :],
                                 start=True, stop=True)

            def power_tile(k, a):
                for t in range(NT):
                    c = slice(a * P, (a + 1) * P)
                    last = mm3(bank[4 + a][:, :], Lns[:, 0, t, c], Lns[:, 1, t, c],
                               LT[:, k - 1, 0, t, :], LT[:, k - 1, 1, t, :], t == 0, t == NT - 1)
                last.then_inc(lt_mm, 1)

            pe.wait_ge(pool_const, 1)
            pe.wait_ge(alpha_in, 16)
            pe.wait_ge(rows_in, 64)
            R = NT + E + 2 + E
            pe.transpose(bank[0][:, 0:R], rows[:, :], ident[0:R, 0:R]).then_inc(rows_t, 1)
            pe.wait_ge(w_in, 16)
            pe.transpose(bank[1][:, 0:P], w_raw[:, 0, :], ident[:, :]).then_inc(w_t, 1)
            pe.wait_ge(wt_ready, 1)
            pe.matmul(bank[2][:, 0:P], wT[:, 1, :], wT[:, 0, :], start=True, stop=True).then_inc(weff_mm, 1)
            for t in range(NT):
                pe.wait_ge(lnat_ready, t + 1)
                for a in range(NT):
                    last = pe.transpose(bank[4 + a][:, t * P:(t + 1) * P], Lnat[:, t, a * P:(a + 1) * P], ident[:, :])
                    if t == NT - 1:
                        last.then_inc(lt_mm, 1)
            pe.wait_ge(pow_ready, 1)
            pe.matmul(bank[3][:, 0:P], Rp[:, 0, :], Rp[:, 0, :], start=True, stop=True).then_inc(pow_mm, 1)
            pe.wait_ge(x0_ready, 1)
            pe.wait_ge(lt_lo, NT)
            transpose_x0(0, 0)
            transpose_x0(0, 1)
            pe.wait_ge(x0_lo, 1)
            nodes_product(0, 0)
            pe.wait_ge(pow_ready, 2)
            pe.matmul(bank[3][:, 0:2 * P], Rp[:, 1, :], Rp[:, 0:2, :], start=True, stop=True).then_inc(pow_mm, 1)
            pe.wait_ge(x0t_lo, GB)
            nodes_product(0, 2)
            pe.wait_ge(pow_ready, 3)
            pe.matmul(bank[1][:, :], Rp[:, 3, :], Rp[:, 0:4, :], start=True, stop=True).then_inc(pow_mm, 1)
            pe.wait_ge(lnat_lo, 1)
            for a in range(NT):
                power_tile(1, a)
            pe.wait_ge(pow_ready, 4)
            pe.wait_ge(gt_lo, 2)
            for c in range(BABY):
                times_powers(bank[CREP_BANK[c]], cols[:, FB_COL:FB_COL + 1].to_broadcast([P, P]), c).then_inc(crep_mm, 1)
            pe.wait_ge(v1_ready, 1)
            for t in range(NT):
                for m in range(NT):
                    for s in range(2):
                        last = pe.matmul(bank[0][:, 2 * t:2 * t + 2], LT[:, 0, s, m, t * P:(t + 1) * P],
                                         ones_v[:, m, :], start=(m == 0 and s == 0), stop=(m == NT - 1 and s == 1))
            last.then_inc(v2_mm, 1)
            pe.wait_ge(lt_lo, 2 * NT)
            pe.wait_ge(crep_ready, BABY)
            nodes_product(0, 1)
            nodes_product(0, 3)
            pe.wait_ge(fc_in, 16)
            pe.wait_ge(v2_read, 1)
            for c in range(BABY):
                times_powers(bank[FR_BANK[c]], w_raw[:, 1, :], c).then_inc(fr_mm, 1)
            for a in range(NT):
                if a == NT - 1:
                    pe.wait_ge(m_sum, BABY)
                power_tile(2, a)

            def horner(src, banks, done, ready, at):
                for p in range(2):
                    pe.wait_ge(ready, at[p])
                    for t in range(NT):
                        yield p, t
                        for m in (2 * p, 2 * p + 1):
                            c = slice(t * P, (t + 1) * P)
                            last = mm3(bank[banks[t]][:, 0:W], LT[:, 2, 0, m, c], LT[:, 2, 1, m, c],
                                       src[:, 0, m], src[:, 1, m], m == 0, m == NT - 1)
                        if p == 1:
                            last.then_inc(done, 1)

            def logits(h):
                pe.wait_ge(zt_lo, GB * h + GB)
                for t in range(T):
                    for s in range(2):
                        c = slice((t // GB) * P, (t // GB + 1) * P)
                        last = pe.matmul(bank[LG_BANK][:, t * C:(t + 1) * C], zT[:, s, t % GB, c], rts[:, :],
                                         start=(s == 0), stop=(s == 1))
                last.then_inc(lg_mm, 1)

            def transpose_comb(h):
                pe.wait_ge(comb_ready, h + 1)
                for b in range(GB):
                    for t in range(NT):
                        last = pe.transpose(bank[CT_BANK[b]][0:C, t * P:(t + 1) * P], cc[:, t * GB + b, :], ident[:, :])
                    last.then_inc(ct_mm, 1)

            def transpose_z(g, b, h=None):
                pe.wait_ge(z_ready, g + 1)
                if b == 1 and h is not None:
                    pe.wait_ge(out_add, 1 + GB * h + 1)
                for t in range(NT):
                    last = pe.transpose(bank[ZT_BANK[b]][:, t * P:(t + 1) * P], z[:, t, b, :], ident[:, :])
                last.then_inc(zt_mm, 1)

            def transpose_out(h, b, g=None):
                pe.wait_ge(yt_copied, GB * h + b + 1)
                if b == 1 and g is not None:
                    pe.wait_ge(zt_lo, GB * g + 1)
                for t in range(NT):
                    last = pe.transpose(bank[OT_BANK[b]][:, t * P:(t + 1) * P], yT[:, t * P:(t + 1) * P], ident[:, :])
                last.then_inc(ot_mm, 1)

            def experts(h, g=None, more=False):
                for s in range(ITEMS + LAG):
                    if s < ITEMS:
                        b, e = s // E, s % E
                        if s >= 2:
                            pe.wait_ge(gelu_done, ITEMS * h + s - 1)
                        elif g is not None:
                            pe.wait_ge(x1_add, NT * g + s + 1)
                        mm3(bank[UP_BANK[s % 2]][:, :], w1s[:, 0, e, :], w1s[:, 1, e, :],
                            zT[:, 0, b, :], zT[:, 1, b, :], True, True).then_inc(up_mm, 1)
                        if s >= 2:
                            pe.wait_ge(sc_ready, ITEMS * h + s - 1)
                        elif g is not None:
                            pe.wait_ge(x1_add, NT * g + s + 3)
                        pe.matmul(bank[REP_BANK[s % 2]][:, :], sel[:, e, :], combT[:, b, :],
                                  start=True, stop=True).then_inc(rep_mm, 1)
                        if e == LAG - 1:
                            for k in range(2):
                                pe.matmul(bank[SUM_BANK[b]][:, :], b2s[:, k, :], combT[:, b, :],
                                          start=(k == 0), stop=False)
                    if s == ITEMS - 1 and g is not None:
                        transpose_z(g, 1, h)
                    if s == ITEMS and more:
                        pe.wait_ge(x0_ready, g + 2)
                        transpose_x0(g + 1, 0)
                    if s == ITEMS + 1 and more:
                        pe.wait_ge(gelu_done, ITEMS * h + ITEMS - 1)
                        transpose_x0(g + 1, 1)
                    i = s - LAG
                    if i >= 0:
                        b, e = i // E, i % E
                        pe.wait_ge(sc_lo, ITEMS * h + i + 1)
                        mm3(bank[SUM_BANK[b]][:, :], w2s[:, 0, e, :], w2s[:, 1, e, :],
                            scs[:, i % RING, 0, :], scs[:, i % RING, 1, :], False, e == E - 1).then_inc(down_mm, 1)
                    if s == E + LAG + 1:
                        transpose_out(h, 0)
                    if s == E + LAG + 2 and g is not None:
                        transpose_z(g, 0)
                if more:
                    pe.wait_ge(x0_lo, g + 2)
                    pe.wait_ge(zt_lo, GB * g + GB)
                    nodes_product(g + 1, 0)
                transpose_out(h, 1, g)
                if more:
                    pe.wait_ge(out_add, 1 + GB * h + GB)
                    nodes_product(g + 1, 1)

            def iteration(g, first=False, final=False):
                if not first:
                    pe.wait_ge(x0t_lo, GB * g + GB)
                    nodes_product(g, 2)
                    logits(g - 1)
                    nodes_product(g, 3)
                else:
                    pe.wait_ge(m_lo, 1)
                for i in range(T):
                    b, t = i // NT, i % NT
                    pe.wait_ge(gt_lo, 2 * GB * g + (2 * GB if first else max(2 * b + 2, min(i + 1, 2 * GB))))
                    if i >= 4:
                        pe.wait_ge(q_ready, T * g + i - 3)
                    dst = bank[GT_BANK[i % 4]][:, 0:BABY * D]
                    c = slice(t * P, (t + 1) * P)
                    for k in range(BABY):
                        last = mm3(dst, GT[:, b, k, 0, c], GT[:, b, k, 1, c], M[:, 0, :, k, :], M[:, 1, :, k, :],
                                   k == 0, k == BABY - 1)
                    last.then_inc(q_mm, 1)
                if first:
                    pe.wait_ge(lt_lo, BABY * NT)
                    pe.wait_ge(small_ready, 2)
                else:
                    transpose_comb(g - 1)
                for p, t in horner(y2s, Y1_BANK, y1_mm, y2_lo, [2 * g + 1, 2 * g + 2]):
                    if p == 0 and t >= 2:
                        pe.wait_ge(q_ready, T * g + NT + t + 1)
                if not first:
                    pe.wait_ge(ct_copied, GB * g)
                for _ in horner(y1s, H8_BANK, h8_mm, y1_lo, [NT * g + 2, NT * g + 4]):
                    pass
                if first:
                    pe.wait_ge(x0_ready, g + 2)
                    transpose_x0(g + 1, 0)
                    pe.wait_ge(x1_add, NT * g + 1)
                    transpose_x0(g + 1, 1)
                    pe.wait_ge(x0_lo, g + 2)
                    nodes_product(g + 1, 0)
                    nodes_product(g + 1, 1)
                    pe.wait_ge(gt_lo, 2 * GB * (g + 1) + 2)
                    for b in range(GB):
                        transpose_z(g, b)
                else:
                    experts(g - 1, g, not final)

            iteration(0, first=True)
            with pe.Fori(1, GROUPS - 1) as g:
                iteration(g)
            iteration(GROUPS - 1, final=True)
            logits(GROUPS - 1)
            transpose_comb(GROUPS - 1)
            pe.wait_ge(ct_copied, GB * GROUPS)
            experts(GROUPS - 1)


_INS = ['x', 'adj', 'L0_gnn_alpha_train', 'L0_gnn_w', 'L0_gnn_d', 'L0_gnn_fc_in_w', 'L0_gnn_fc_in_b',
        'L0_ffn_router_w', 'L0_ffn_w1', 'L0_ffn_b1', 'L0_ffn_w2', 'L0_ffn_b2']


def kernel(**inputs):
    import numpy as _np
    import concourse.bacc as _bacc
    from concourse import mybir as _mybir
    from concourse.bass_utils import run_bass_kernel_spmd as _run

    nc = _bacc.Bacc("TRN2", target_bir_lowering=False, num_devices=1)
    arrays, args = {}, []
    for name in _INS:
        a = _np.ascontiguousarray(inputs[name])
        arrays[f"in_{name}_dram"] = a
        args.append(nc.dram_tensor(f"in_{name}_dram", a.shape, _mybir.dt.from_np(a.dtype), kind="ExternalInput").ap())
    shape = arrays["in_x_dram"].shape
    args.append(nc.dram_tensor("out_0_dram", shape, _mybir.dt.float32, kind="ExternalOutput").ap())
    build(nc, *args)
    r = _run(nc, [arrays], core_ids=[0])
    return r.results[0]["out_0_dram"]
```

```python
import concourse.bass as bass
from concourse import mybir
from contextlib import ExitStack
from math import comb as binomial

FP32 = mybir.dt.float32
F32R = mybir.dt.float32r
I32 = mybir.dt.int32
ALU = mybir.AluOpType
ACT = mybir.ActivationFunctionType
AX = mybir.AxisListType

P = 128
STEPS = 8
DT = 1.0 / STEPS
EPS = 1e-5
BABY = 3
LAG = 5
LOW_DVE = (3, 4, 8, 15)
RING = 6


def build(nc, x, adj, alpha, w, d, fc_w, fc_b, router_w, w1, b1, w2, b2, comb_rows, out):
    B, N, D = x.shape
    E = router_w.shape[0]
    NT = N // P
    GB = 2
    GROUPS = B // GB
    T = NT * GB
    ITEMS = GB * E
    W = GB * D
    C = 2 * E
    V = 5 * E
    K = STEPS + 1
    assert D == P and K == BABY * BABY and N == 512

    ctx = ExitStack()
    with ctx:
        def sb(name, shape, dt=FP32):
            return ctx.enter_context(nc.sbuf_tensor(name, shape, dt))

        def sem(name):
            return ctx.enter_context(nc.semaphore(name))

        ident = sb("ident", [P, P])
        alpha_rows = sb("alpha_rows", [NT, P])
        rows = sb("rows", [E + 2 + E, P])
        cols = sb("cols", [P, NT + E + 2 + E])
        A_COL, B1_COL, D_COL, FB_COL, RT_COL = 0, NT, NT + E, NT + E + 1, NT + E + 2
        node = sb("node", [P, 6, NT])
        ones = sb("ones", [P, P], F32R)
        dclip = sb("dclip", [P, 1])
        LT = sb("LT", [P, BABY, 2, NT, N], F32R)
        M = sb("M", [P, 2, BABY, BABY, D], F32R)
        bias = sb("bias", [P, NT, BABY, D])
        w1s = sb("w1s", [P, 2, E, D], F32R)
        w2s = sb("w2s", [P, 2, E, D], F32R)
        b2s = sb("b2s", [GB * V, GB, D], F32R)
        rts = sb("rts", [P, C], F32R)
        pick = sb("pick", [GB * V, C], F32R)
        rank_i = sb("rank_i", [P, T, E], I32)
        rank = sb("rank", [P, T, E])
        nhalf = sb("nhalf", [P, T])

        xn = sb("xn", [P, NT, GB, D])
        xg = sb("xg", [P, NT, GB, D])
        x0 = sb("x0", [P, NT, GB, D])
        x0s = sb("x0s", [P, 2, NT, GB, D], F32R)
        GT = sb("GT", [P, GB, BABY, 2, N], F32R)
        y1s = GT[:, 1].rearrange("p i s n -> p (i s n)")[:, 0:2 * T * D] \
            .rearrange("p (s t b c) -> p s t b c", s=2, t=NT, b=GB)
        Q = sb("Q", [P, BABY, NT, GB, D])
        y1 = Q[:, 2]
        x1 = Q[:, 0]
        w12_raw = Q[:, 0:2].rearrange("p k t b c -> p k (t b) c")
        Rp = Q[:, 2].rearrange("p t b c -> p (t b) c")
        scr = sb("scr", [P, 2, K, D])
        SK = scr[:, 0]
        crep = scr[:, 1]
        z = scr[:, 0, 0:T, :].rearrange("p (t b) c -> p t b c", b=GB)
        res = scr[:, 1, 0:T, :].rearrange("p (t b) c -> p t b c", b=GB)
        bn = sb("bn", [P, 2, T, 6])
        mv = sb("mv", [P, 2, 3, T])
        ve = sb("ve", [P, 2, T])
        rstd = sb("rstd", [P, 2, T])
        zT = sb("zT", [P, 2, GB, N], F32R)
        zT_next = sb("zT_next", [P, 2, N], F32R)
        rt = sb("rt", [P, 6, T, E])
        rm = sb("rm", [P, 10, T])
        cc = sb("cc", [P, T, 5, E])
        combT = sb("combT", [GB * V, N], F32R)
        comb_out = sb("comb_out", [GB * V, N])
        work = sb("work", [P, 5, N])
        hid = work[:, 0:2]
        scaled = work[:, 2:5]
        Lnat = work[:, 0:4]
        w_raw = work[:, 4, 0:2 * P].rearrange("p (k c) -> p k c", c=P)
        wT = work[:, 4, 2 * P:4 * P].rearrange("p (k c) -> p k c", c=P)
        scs = sb("scs", [P, RING, 2, N], F32R)
        Lns = scs[:, 0:NT, :, :].rearrange("p r s n -> p s r n")
        y2s = scs[:, 0:NT].rearrange("p r s n -> p (r s n)")[:, 0:2 * T * D] \
            .rearrange("p (s t b c) -> p s t b c", s=2, t=NT, b=GB)
        yT = sb("yT", [P, N])
        outs = sb("outs", [P, GB, NT, D])
        b2_raw = yT[0:GB * V, :].rearrange("p (s b c) -> p s b c", s=2, c=D)
        b2_high = outs[0:GB * V, 0, 0:GB, :]
        ident_dt = outs[:, 0, GB, :]
        v2_diag = outs[:, 1]

        def rep(i):
            if i % E < 6:
                return GT[:, i // E].rearrange("p i s n -> p (i s) n")[:, i % E, :].bitcast(FP32)
            return Q[:, 1 + i // E].rearrange("p t b c -> p (t b c)").rearrange("p (r n) -> p r n", n=N)[:, i % E - 6, :]

        bank = [ctx.enter_context(nc.psum_tensor(f"bank{i}", [P, 512], FP32)) for i in range(8)]

        rows_in, alpha_in, w_in, fc_in, w12_in, b2_in = (
            sem(n) for n in ("rows_in", "alpha_in", "w_in", "fc_in", "w12_in", "b2_in"))
        adj_in = [sem(f"adj_in{t}") for t in range(NT)]
        adj_scaled = sem("adj_scaled")
        pool_const, pool_own = sem("pool_const"), sem("pool_own")
        rows_t, w_t, cols_ready, sig_exp = sem("rows_t"), sem("w_t"), sem("cols_ready"), sem("sig_exp")
        node_ready = sem("node_ready")
        set_own = sem("set_own")
        lnat_ready, lnat_hi, lnat_lo = sem("lnat_ready"), sem("lnat_hi"), sem("lnat_lo")
        wt_ready, weff_mm = sem("wt_ready"), sem("weff_mm")
        pow_mm, pow_ready = sem("pow_mm"), sem("pow_ready")
        lt_mm, lt_hi, lt_lo = sem("lt_mm"), sem("lt_hi"), sem("lt_lo")
        fr_mm, crep_mm, crep_ready = sem("fr_mm"), sem("crep_mm"), sem("crep_ready")
        m_sum, m_hi, m_lo = sem("m_sum"), sem("m_hi"), sem("m_lo")
        ones_ready, v2_mm, v2_read = sem("ones_ready"), sem("v2_mm"), sem("v2_read")
        wsp_hi, wsp_lo = sem("wsp_hi"), sem("wsp_lo")
        small_ready, b2_zero = sem("small_ready"), sem("b2_zero")

        x_in = [sem(f"x_in{b}") for b in range(GB)]
        xg_copied = sem("xg_copied")
        ln_own = [sem("ln1_own"), sem("ln2_own")]
        ln_ve = [sem("ln1_ve"), sem("ln2_ve")]
        ln_rstd = [sem("ln1_rstd"), sem("ln2_rstd")]
        x0_ready = sem("x0_ready")
        x0_hi, x0_lo = sem("x0_hi"), sem("x0_lo")
        x0t_mm, x0t_hi, x0t_lo = sem("x0t_mm"), sem("x0t_hi"), sem("x0t_lo")
        gt_mm, gt_hi, gt_lo = sem("gt_mm"), sem("gt_hi"), sem("gt_lo")
        q_mm, q_ready = sem("q_mm"), sem("q_ready")
        y2_hi, y2_lo = sem("y2_hi"), sem("y2_lo")
        y1_mm, y1_add = sem("y1_mm"), sem("y1_add")
        y1_hi, y1_lo = sem("y1_hi"), sem("y1_lo")
        xq_ready = sem("xq_ready")
        h8_mm, x1_add = sem("h8_mm"), sem("x1_add")
        z_ready, res_ready = sem("z_ready"), sem("res_ready")
        zt_mm, zt_hi, zt_lo = sem("zt_mm"), sem("zt_hi"), sem("zt_lo")
        zt_moved = sem("zt_moved")
        lg_mm, rt_own, rt_pre, rt_exp, comb_ready = (sem(n) for n in ("lg_mm", "rt_own", "rt_pre", "rt_exp", "comb_ready"))
        rep_mm = sem("rep_mm")
        ct_mm, ct_copied, ct_high = sem("ct_mm"), sem("ct_copied"), sem("ct_high")
        comb_stored = sem("comb_stored")
        rep_in = [sem(f"rep_in{k}") for k in range(5)]
        up_mm, gelu_done, sc_ready = sem("up_mm"), sem("gelu_done"), sem("sc_ready")
        sc_hi, down_mm = sem("sc_hi"), sem("down_mm")
        sc_lo_pool, sc_lo_dve = sem("sc_lo_pool"), sem("sc_lo_dve")
        yt_copied, ot_mm = sem("yt_copied"), sem("ot_mm")
        out_add = sem("out_add")
        out_stored = sem("out_stored")
        LN_OWN = T + 2
        RT_OWN = 23

        GT_BANK = [2, 3, 0, 1]
        Y1_BANK = [2, 3, 0, 1]
        H8_BANK = [4, 5, 6, 7]
        REP_ITEMS = [0, 2, 6, 8, 14]
        REP_BANK, REP_PE = [3, 7], 6
        Z_ITEM = 11
        UP_BANK, SUM_BANK = [4, 5, 6], [0, 1]
        X0_BANK, X0_SETUP = [0, 5], [6, 7]
        CREP_BANK, FR_BANK, V2_BANK = [1, 2, 3], [2, 0, 7], 2
        ZT_BANK, OT_BANK, LG_BANK, CT_BANK = [7, 3], [2, 6], 7, 7

        x_v = x.rearrange("(g b) (t p) c -> g b p t c", b=GB, p=P)
        out_v = out.rearrange("(g b) (t p) c -> g b p t c", b=GB, p=P)

        def of_group(v, g, b):
            return v[bass.ds(g, 1), b, :, :, :].rearrange("o p t c -> p (o t) c")

        def q_tile(i):
            return (i // 2) % GB, 2 * (i // 4) + i % 2

        def zt_part(s, b):
            return zT_next[:, s, :] if b == GB - 1 else zT[:, s, b, :]

        def wait_low(engine, h, i):
            by_dve = sum(k <= i for k in LOW_DVE)
            if i in LOW_DVE:
                engine.wait_ge(sc_lo_dve, len(LOW_DVE) * h + by_dve)
            else:
                engine.wait_ge(sc_lo_pool, (ITEMS - len(LOW_DVE)) * h + i + 1 - by_dve)

        block = ctx.enter_context(nc.Block())

        @block.sync
        def _(sp):
            sp.sem_inc(out_add, 1)
            sp.sem_inc(out_stored, 1)
            sp.dma_start(alpha_rows[:, :], alpha.rearrange("(t p) -> t p", p=P)).then_inc(alpha_in, 16)

            def load_x(g):
                for b in range(GB):
                    sp.dma_start(xn[:, :, b, :], of_group(x_v, g, b)).then_inc(x_in[b], 16)

            def next_x(g):
                sp.wait_ge(x0_ready, g)
                sp.wait_ge(xg_copied, g)
                load_x(g)

            def store(h):
                for b in range(GB):
                    sp.wait_ge(out_add, 1 + GB * h + b + 1)
                    sp.dma_start(of_group(out_v, h, b), outs[:, b, :, :]).then_inc(out_stored, 16)

            load_x(0)
            for t in range(NT):
                sp.dma_start(Lnat[:, t, :], adj[t * P:(t + 1) * P, :]).then_inc(adj_in[t], 16)
            sp.dma_start(w_raw[:, 0, :], w).then_inc(w_in, 16)
            for k, src in ((D_COL, d), (FB_COL, fc_b)):
                sp.dma_start(rows[k - NT:k - NT + 1, :], src.rearrange("(o p) -> o p", o=1)).then_inc(rows_in, 16)
            for k, src in ((B1_COL, b1), (RT_COL, router_w)):
                sp.dma_start(rows[k - NT:k - NT + E, :], src).then_inc(rows_in, 16)
            sp.dma_start(w_raw[:, 1, :], fc_w).then_inc(fc_in, 16)
            sp.dma_start(w12_raw[:, 0], w1.rearrange("e c f -> c e f")).then_inc(w12_in, 16)
            sp.dma_start(w12_raw[:, 1], w2.rearrange("e f c -> f e c")).then_inc(w12_in, 16)
            sp.wait_ge(b2_zero, 1)
            for b in range(GB):
                for k in range(4):
                    r = b * V + k * E
                    sp.dma_start(b2_raw[r:r + E, k // 2, b, :], b2).then_inc(b2_in, 16)

            def replicate(h, k, count, b, e):
                first = rep(b * E + e)
                dst = bass.AP(first.tensor, first.offset, [list(first.ap[0]), [N, count], [1, N]])
                src = comb_rows[bass.ds(h, 1), b, e:e + count, :].rearrange("o e n -> (o e) n").partition_broadcast(P)
                sp.dma_start(dst, src).then_inc(rep_in[k], 16)

            def expert_weights(h, g=None):
                sp.wait_ge(ct_copied, h + 1)
                for b in range(GB):
                    sp.dma_start(comb_rows[bass.ds(h, 1), b, :, :].rearrange("o e n -> (o e) n"),
                                 comb_out[b * V + 4 * E:(b + 1) * V, :]).then_inc(comb_stored, 16)
                if g is not None:
                    sp.wait_ge(q_ready, T * g + T)
                else:
                    sp.wait_ge(sc_ready, ITEMS * h)
                sp.wait_ge(comb_stored, 32 * h + 32)
                if g is not None:
                    replicate(h, 0, 2, 0, 0)
                    replicate(h, 1, 4, 0, 2)
                    sp.wait_ge(y1_add, NT * g + NT)
                replicate(h, 2, 2, 0, 6)
                if g is not None:
                    sp.wait_ge(h8_mm, NT * g + NT)
                replicate(h, 3, 6, 1, 0)
                replicate(h, 4, 2, 1, 6)

            next_x(1)
            next_x(2)
            with sp.Fori(1, GROUPS - 2) as g:
                expert_weights(g - 1, g)
                next_x(g + 2)
                store(g - 1)
            for g in range(GROUPS - 2, GROUPS):
                expert_weights(g - 1, g)
                store(g - 1)
            expert_weights(GROUPS - 1)
            store(GROUPS - 1)
            sp.wait_ge(out_stored, 1 + 32 * GROUPS)

        @block.gpsimd
        def _(pool):
            nc.gpsimd.memset(ident[:, :], 0.0).then_inc(pool_own, 1)
            pool.wait_ge(pool_own, 1)
            nc.gpsimd.affine_select(out=ident[:, :], in_=ident[:, :], compare_op=ALU.not_equal, fill=1.0,
                                    base=0, pattern=[[-1, P]], channel_multiplier=1).then_inc(pool_const, 1)
            nc.gpsimd.iota(rank_i[:, :, :], pattern=[[0, T], [-1, E]], base=E, channel_multiplier=0)
            nc.gpsimd.memset(b2_raw, 0.0).then_inc(b2_zero, 1)
            nc.gpsimd.memset(nhalf[:, :], -0.5).then_inc(pool_own, 1)
            pool.wait_ge(pool_own, 2)
            nc.gpsimd.tensor_copy(rank[:, :, :], rank_i[:, :, :]).then_inc(pool_const, 1)

            def inverse_root(n, g):
                pool.wait_ge(ln_ve[n], g + 1)
                nc.gpsimd.tensor_tensor(rstd[:, n, :], ve[:, n, :], nhalf[:, :], ALU.pow).then_inc(ln_rstd[n], 1)

            def low_x0(g):
                for b in range(GB):
                    pool.wait_ge(x0_hi, GB * g + b + 1)
                    nc.gpsimd.tensor_tensor(x0s[:, 1, :, b], x0[:, :, b], x0s[:, 0, :, b].bitcast(FP32),
                                            ALU.subtract).then_inc(x0_lo, 1)

            def item_low(h, i):
                pool.wait_ge(sc_hi, ITEMS * h + i + 1)
                nc.gpsimd.tensor_tensor(scs[:, i % RING, 1, :], scaled[:, i % 3, :],
                                        scs[:, i % RING, 0, :].bitcast(FP32), ALU.subtract).then_inc(sc_lo_pool, 1)

            def residual(h):
                pool.wait_ge(z_ready, h + 1)
                pool.wait_ge(out_add, 1 + GB * h)
                nc.gpsimd.tensor_tensor(res, x1, z, ALU.add).then_inc(res_ready, 1)

            inverse_root(0, 0)
            pool.wait_ge(lnat_hi, 1)
            nc.gpsimd.tensor_tensor(Lns[:, 1], Lnat, Lns[:, 0].bitcast(FP32), ALU.subtract).then_inc(lnat_lo, 1)
            for k in range(2):
                pool.wait_ge(wsp_hi, k + 1)
                nc.gpsimd.tensor_tensor((w1s, w2s)[k][:, 1], w12_raw[:, k],
                                        (w1s, w2s)[k][:, 0].bitcast(FP32), ALU.subtract).then_inc(wsp_lo, 1)

            def iteration(g, first=False, final=False):
                if not first:
                    residual(g - 1)
                if not final:
                    inverse_root(0, g + 1)
                pool.wait_ge(xg_copied, g + 1)
                pool.wait_ge(q_ready, T * g + T)
                nc.gpsimd.tensor_tensor(Q[:, 0], Q[:, 0], xg[:, :, :, :], ALU.add).then_inc(xq_ready, 1)
                if not final:
                    low_x0(g + 1)
                if first:
                    inverse_root(1, g)
                else:
                    for i in range(ITEMS):
                        if i not in LOW_DVE:
                            item_low(g - 1, i)
                        if i == 2:
                            inverse_root(1, g)

            iteration(0, first=True)
            with pool.Fori(1, GROUPS - 1) as g:
                iteration(g)
            iteration(GROUPS - 1, final=True)
            residual(GROUPS - 1)
            for i in range(ITEMS):
                if i not in LOW_DVE:
                    item_low(GROUPS - 1, i)

        @block.scalar
        def _(act):
            def high(dst, src):
                return nc.scalar.activation(dst, src, ACT.Copy)

            act.wait_ge(cols_ready, 1)
            nc.scalar.activation(node[:, 0, :], cols[:, A_COL:A_COL + NT], ACT.Exp, scale=-1.0).then_inc(sig_exp, 1)

            def high_x0(g):
                act.wait_ge(x0_ready, g + 1)
                for b in range(GB):
                    high(x0s[:, 0, :, b], x0[:, :, b]).then_inc(x0_hi, 1)

            def copy_x(g):
                act.wait_ge(x0_ready, g + 1)
                if not (isinstance(g, int) and g == 0):
                    act.wait_ge(xq_ready, g)
                high(xg[:, :, :, :], xn[:, :, :, :]).then_inc(xg_copied, 1)

            def high_x0t(g, banks=X0_BANK):
                for b in range(GB):
                    act.wait_ge(x0t_mm, GB * g + b + 1)
                    high(GT[:, b, 0, 0, :], bank[banks[b]][:, :]).then_inc(x0t_hi, 1)

            def high_gt(g, k, turn):
                act.wait_ge(gt_mm, 2 * GB * g + turn + 1)
                high(GT[:, k // 2, 1 + k % 2, 0, :], bank[GT_BANK[k]][:, :]).then_inc(gt_hi, 1)

            def high_lt(k, tiles=range(NT)):
                for a in tiles:
                    act.wait_ge(lt_mm, NT * k + a + 1)
                    high(LT[:, k, 0, a, :], bank[4 + a][:, :]).then_inc(lt_hi, 1)

            act.wait_ge(node_ready, 1)
            for t in range(NT):
                act.wait_ge(adj_in[t], 16)
                nc.scalar.activation(Lnat[:, t, :], Lnat[:, t, :], ACT.Copy,
                                     scale=node[:, 3, t:t + 1]).then_inc(adj_scaled, 1)
            high_lt(0, [0])
            high_x0(0)
            high_lt(0, range(1, NT))
            act.wait_ge(lnat_ready, NT)
            high(Lns[:, 0], Lnat).then_inc(lnat_hi, 1)
            copy_x(0)
            high_gt(0, 0, 0)
            high_gt(0, 2, 1)
            high_x0t(0, X0_SETUP)
            high_lt(1)
            act.wait_ge(w12_in, 32)
            high(w1s[:, 0], w12_raw[:, 0]).then_inc(wsp_hi, 1)
            high(w2s[:, 0], w12_raw[:, 1]).then_inc(wsp_hi, 1)
            high_gt(0, 1, 2)
            high_gt(0, 3, 3)
            act.wait_ge(m_sum, BABY)
            high(M[:, 0], SK.rearrange("p (j i) c -> p j i c", i=BABY)).then_inc(m_hi, 1)
            high_lt(2)

            def copy_sum(h, b):
                act.wait_ge(down_mm, ITEMS * h + E * (b + 1))
                if b:
                    act.wait_ge(ot_mm, GB * h + b)
                high(yT[:, :], bank[SUM_BANK[b]][:, :]).then_inc(yt_copied, 1)

            def high_z(g, b):
                act.wait_ge(zt_mm, GB * g + b + 1)
                high(zt_part(0, b), bank[ZT_BANK[b]][:, :]).then_inc(zt_hi, 1)

            def route_exp(h):
                act.wait_ge(rt_pre, h + 1)
                nc.scalar.activation(rt[:, 1], rt[:, 0], ACT.Exp).then_inc(rt_exp, 1)

            def move_zt(h):
                act.wait_ge(zt_lo, GB * h + GB)
                high(zT[:, :, GB - 1, :], zT_next[:, :, :]).then_inc(zt_moved, 1)

            def copy_comb(h):
                act.wait_ge(ct_mm, h + 1)
                if not (isinstance(h, int) and h == 0):
                    act.wait_ge(comb_stored, 32 * h)
                high(comb_out[:, :], bank[CT_BANK][0:GB * V, :]).then_inc(ct_copied, 1)
                high(combT[:, :], bank[CT_BANK][0:GB * V, :]).then_inc(ct_high, 1)

            def item_high(h, i):
                act.wait_ge(sc_ready, ITEMS * h + i + 1)
                if i >= RING:
                    act.wait_ge(down_mm, ITEMS * h + i - RING + 1)
                high(scs[:, i % RING, 0, :], scaled[:, i % 3, :]).then_inc(sc_hi, 1)

            def experts(h, g=None, more=False):
                for i in range(ITEMS):
                    act.wait_ge(up_mm, ITEMS * h + i + 1)
                    if i >= 2:
                        act.wait_ge(sc_ready, ITEMS * h + i - 1)
                    e = i % E
                    nc.scalar.activation(hid[:, i % 2, :], bank[UP_BANK[i % 3]][:, :], ACT.Gelu,
                                         bias=cols[:, B1_COL + e:B1_COL + e + 1]).then_inc(gelu_done, 1)
                    if i == 1 and g is None:
                        copy_comb(h)
                    if i >= 1:
                        item_high(h, i - 1)
                    if i == Z_ITEM + 1 and g is not None:
                        high_z(g, 0)
                    if i == ITEMS - 3:
                        copy_sum(h, 0)
                    if i == Z_ITEM + 2 and g is not None:
                        high_z(g, 1)
                item_high(h, ITEMS - 1)
                if g is not None:
                    route_exp(g)
                if more:
                    high_x0t(g + 1)
                copy_sum(h, 1)

            def iteration(g, first=False, final=False):
                if not first:
                    move_zt(g - 1)
                    high_gt(g, 3, 3)
                for p in range(2):
                    act.wait_ge(q_ready, T * g + NT * (p + 1))
                    high(y2s[:, 0, 2 * p:2 * p + 2], Q[:, 2, 2 * p:2 * p + 2]).then_inc(y2_hi, 1)
                    if p == 0 and not first:
                        copy_comb(g - 1)
                if not final:
                    high_x0(g + 1)
                for t in range(NT):
                    act.wait_ge(y1_add, NT * g + t + 1)
                    high(y1s[:, 0, t], y1[:, t]).then_inc(y1_hi, 1)
                if not final:
                    copy_x(g + 1)
                if first:
                    high_x0t(g + 1)
                    for k in range(2):
                        high_gt(g + 1, k, k)
                    for b in range(GB):
                        high_z(g, b)
                    high_gt(g + 1, 2, 2)
                    route_exp(g)
                else:
                    experts(g - 1, g, not final)
                    if not final:
                        for k in range(3):
                            high_gt(g + 1, k, k)

            iteration(0, first=True)
            with act.Fori(1, GROUPS - 1) as g:
                iteration(g)
            iteration(GROUPS - 1, final=True)
            move_zt(GROUPS - 1)
            experts(GROUPS - 1)

        @block.vector
        def _(dve):
            v = nc.vector

            def low(dst, src, hi):
                return v.tensor_tensor(dst, src, hi.bitcast(FP32), ALU.subtract)

            def ln_stats(n, g, src, t):
                v.bn_stats(bn[:, n, t, :], src[:, t // GB, t % GB, :]).then_inc(ln_own[n], 1)

            def ln_var(n, g):
                mean_e, mean_o = bn[:, n, :, 1], bn[:, n, :, 4]
                dve.wait_ge(ln_own[n], LN_OWN * g + T)
                v.tensor_tensor(mv[:, n, 1, :], mean_e, mean_o, ALU.subtract)
                v.tensor_tensor(mv[:, n, 2, :], bn[:, n, :, 2], bn[:, n, :, 5], ALU.add)
                v.tensor_tensor(mv[:, n, 0, :], mean_e, mean_o, ALU.add).then_inc(ln_own[n], 1)
                dve.wait_ge(ln_own[n], LN_OWN * g + T + 1)
                v.tensor_tensor(mv[:, n, 1, :], mv[:, n, 1, :], mv[:, n, 1, :], ALU.mult)
                v.tensor_scalar(mv[:, n, 0, :], mv[:, n, 0, :], 0.5, None, ALU.mult)
                v.tensor_scalar(mv[:, n, 2, :], mv[:, n, 2, :], 1.0 / D, EPS, ALU.mult, ALU.add).then_inc(ln_own[n], 1)
                dve.wait_ge(ln_own[n], LN_OWN * g + T + 2)
                v.scalar_tensor_tensor(out=ve[:, n, :], in0=mv[:, n, 1, :], scalar=0.25, in1=mv[:, n, 2, :],
                                       op0=ALU.mult, op1=ALU.add).then_inc(ln_ve[n], 1)

            def ln_scale(n, dst, src, t):
                return v.tensor_scalar(dst[:, t // GB, t % GB, :], src[:, t // GB, t % GB, :],
                                       mv[:, n, 0, t:t + 1], rstd[:, n, t:t + 1], ALU.subtract, ALU.mult)

            def norm_x_stats(g, b):
                dve.wait_ge(x_in[b], 16 * g + 16)
                for t in range(NT):
                    ln_stats(0, g, xn, t * GB + b)

            def norm_x_scale(g, part, parts):
                if part == 0:
                    dve.wait_ge(ln_rstd[0], g + 1)
                for t in range(T * part // parts, T * (part + 1) // parts):
                    last = ln_scale(0, x0, xn, t)
                if part == parts - 1:
                    last.then_inc(x0_ready, 1)

            own = [0]

            def step(ins):
                own[0] += 1
                ins.then_inc(set_own, 1)
                dve.wait_ge(set_own, own[0])

            def low_lt(k, tiles=range(NT)):
                for a in tiles:
                    dve.wait_ge(lt_hi, NT * k + a + 1)
                    low(LT[:, k, 1, a, :], bank[4 + a][:, :], LT[:, k, 0, a, :]).then_inc(lt_lo, 1)

            def low_x0t(g, b, banks=X0_BANK):
                dve.wait_ge(x0t_hi, GB * g + b + 1)
                low(GT[:, b, 0, 1, :], bank[banks[b]][:, :], GT[:, b, 0, 0, :]).then_inc(x0t_lo, 1)

            def low_gt(g, k, turn):
                dve.wait_ge(gt_hi, 2 * GB * g + turn + 1)
                low(GT[:, k // 2, 1 + k % 2, 1, :], bank[GT_BANK[k]][:, :],
                    GT[:, k // 2, 1 + k % 2, 0, :]).then_inc(gt_lo, 1)

            def power_out(n, first, count, src):
                dve.wait_ge(pow_mm, n)
                v.tensor_copy(Rp[:, first - 1:first - 1 + count, :],
                              src[:, 0:count * P].rearrange("p (k c) -> p k c", c=P)).then_inc(pow_ready, 1)

            dve.wait_ge(rows_t, 1)
            v.tensor_copy(cols[:, 0:NT], bank[0][:, 0:NT]).then_inc(cols_ready, 1)
            dve.wait_ge(sig_exp, 1)
            step(v.tensor_scalar(node[:, 1, :], node[:, 0, :], 1.0, None, ALU.add))
            step(v.reciprocal(node[:, 2, :], node[:, 1, :]))
            v.tensor_scalar(node[:, 3, :], node[:, 2, :], DT * 0.5, None, ALU.mult).then_inc(node_ready, 1)
            step(v.tensor_scalar(node[:, 0, :], node[:, 2, :], -DT * 0.5, 1.0 - DT, ALU.mult, ALU.add))
            for b in range(GB):
                norm_x_stats(0, b)
            ln_var(0, 0)
            dve.wait_ge(pool_const, 1)

            def diagonal(t):
                dve.wait_ge(adj_scaled, t + 1)
                diag = Lnat[:, t, t * P:(t + 1) * P]
                v.scalar_tensor_tensor(out=diag, in0=ident[:, :], scalar=node[:, 0, t:t + 1],
                                       in1=diag, op0=ALU.mult, op1=ALU.add).then_inc(lnat_ready, 1)

            for t in range(NT):
                diagonal(t)
            v.tensor_copy(pick[:, :], ident[0:GB * V, 0:C])
            norm_x_scale(0, 0, 1)
            low_lt(0, [0])
            for b in range(GB):
                dve.wait_ge(x0_hi, b + 1)
                low(x0s[:, 1, :, b], x0[:, :, b], x0s[:, 0, :, b]).then_inc(x0_lo, 1)
                low_lt(0, [b + 1])
            low_lt(0, range(GB + 1, NT))
            dve.wait_ge(rows_t, 2)
            dve.wait_ge(w_t, 1)
            v.tensor_copy(cols[:, NT:], bank[1][:, 2 * P:2 * P + E + 2 + E]).then_inc(cols_ready, 1)
            dve.wait_ge(cols_ready, 2)
            step(v.tensor_scalar(dclip[:, :], cols[:, D_COL:D_COL + 1], 0.0, 1.0, ALU.max, ALU.min))
            v.tensor_copy(wT[:, 0, :], bank[1][:, 0:P])
            v.tensor_scalar(wT[:, 1, :], bank[1][:, 0:P], dclip[:, :], None, ALU.mult).then_inc(wt_ready, 1)
            v.tensor_scalar(ident_dt, ident[:, :], DT, None, ALU.mult)
            v.tensor_scalar(ones[:, :], ident[:, :], 0.0, 1.0, ALU.mult, ALU.add).then_inc(ones_ready, 1)
            dve.wait_ge(weff_mm, 1)
            v.tensor_scalar(Rp[:, 0, :], bank[1][:, P:2 * P], DT, None, ALU.mult).then_inc(pow_ready, 1)
            low_gt(0, 0, 0)
            low_gt(0, 2, 1)
            power_out(1, 2, 1, bank[3])
            for b in range(GB):
                low_x0t(0, b, X0_SETUP)
            step(v.tensor_reduce(node[:, 4, :], Lnat, AX.X, ALU.add))
            power_out(2, 3, 2, bank[3])
            low_lt(1, [0])
            power_out(3, 5, 4, bank[1])

            def sum_powers(i):
                for k in range(STEPS - i):
                    last = v.scalar_tensor_tensor(out=SK[:, k, :], in0=Rp[:, i - 1, :], scalar=DT * binomial(k + i, i),
                                                  in1=ident_dt if i == 1 else SK[:, k, :],
                                                  op0=ALU.mult, op1=ALU.add)
                step(last)

            dve.wait_ge(pow_ready, 4)
            sum_powers(1)
            low_lt(1, [1])
            sum_powers(2)
            low_lt(1, [2])
            for c in range(BABY):
                dve.wait_ge(crep_mm, c + 1)
                for r in range(BABY):
                    k = STEPS - (BABY * c + r)
                    last = v.tensor_scalar(crep[:, k, :], bank[CREP_BANK[c]][:, r * D:(r + 1) * D],
                                           float(binomial(STEPS, k)), None, ALU.mult)
                last.then_inc(crep_ready, 1)
            sum_powers(3)
            low_lt(1, [3])
            for i in range(4, STEPS):
                sum_powers(i)
            step(v.tensor_copy(rts[:, 0:E], cols[:, RT_COL:RT_COL + E]))
            low(rts[:, E:C], cols[:, RT_COL:RT_COL + E], rts[:, 0:E])
            dve.wait_ge(b2_in, 16 * 4 * GB)
            step(v.tensor_copy(b2_high.bitcast(F32R), b2_raw[:, 1]))
            step(v.tensor_tensor(b2_high, b2_raw[:, 1], b2_high, ALU.subtract))
            step(v.tensor_copy(b2s[:, :, :], b2_raw[:, 0]))
            v.tensor_tensor(b2s[:, :, :], b2s[:, :, :].bitcast(FP32), b2_high, ALU.add).then_inc(small_ready, 1)
            for c in range(BABY):
                dve.wait_ge(fr_mm, c + 1)
                for r in range(BABY):
                    k = STEPS - (BABY * c + r)
                    src = bank[FR_BANK[c]][:, r * D:(r + 1) * D]
                    if k == STEPS:
                        last = v.tensor_copy(SK[:, k, :], src)
                    else:
                        last = v.scalar_tensor_tensor(out=SK[:, k, :], in0=src, scalar=float(binomial(STEPS, k)),
                                                      in1=ident_dt if k == STEPS - 1 else SK[:, k, :],
                                                      op0=ALU.mult, op1=ALU.add)
                last.then_inc(m_sum, 1)
                if c > 0:
                    low_gt(0, 2 * c - 1, 1 + c)
            dve.wait_ge(m_hi, 1)
            low(M[:, 1], SK.rearrange("p (j i) c -> p j i c", i=BABY), M[:, 0]).then_inc(m_lo, 1)
            low_lt(2, [0])

            def bias_term(i):
                cj = crep.rearrange("p (j i) c -> p j i c", i=BABY)
                for t in range(NT):
                    last = v.scalar_tensor_tensor(out=bias[:, t], in0=cj[:, :, i, :], scalar=node[:, 3 + i, t:t + 1],
                                                  in1=cj[:, :, 0, :] if i == 1 else bias[:, t],
                                                  op0=ALU.mult, op1=ALU.add)
                step(last)

            dve.wait_ge(crep_ready, BABY)
            bias_term(1)
            dve.wait_ge(v2_mm, 1)
            v.tensor_tensor(v2_diag, bank[V2_BANK][:, :].rearrange("p (t c) -> p t c", c=P),
                            ident[:, :].unsqueeze(1).to_broadcast([P, NT, P]), ALU.mult).then_inc(v2_read, 1)
            dve.wait_ge(v2_read, 1)
            step(v.tensor_reduce(node[:, 5, :], v2_diag, AX.X, ALU.add))
            bias_term(2)
            low_lt(2, range(1, NT))

            def per_token(k):
                return rm[:, k, :].unsqueeze(2).to_broadcast([P, T, E])

            def twice(a):
                return a.unsqueeze(2).to_broadcast([P, T, 2, E])

            def routed(h, n, ins):
                ins.then_inc(rt_own, 1)
                dve.wait_ge(rt_own, RT_OWN * h + n)

            def route_start(h):
                dve.wait_ge(lg_mm, h + 1)
                lg = bank[LG_BANK][:, 0:T * C].rearrange("p (t s e) -> p t e s", s=2, e=E)
                routed(h, 1, v.tensor_reduce(rt[:, 2], lg, AX.X, ALU.add))
                routed(h, 2, v.tensor_reduce(rm[:, 0, :], rt[:, 2], AX.X, ALU.max))
                v.tensor_tensor(rt[:, 0], rt[:, 2], per_token(0), ALU.subtract).then_inc(rt_pre, 1)

            def route_on(h, part):
                if part == 0:
                    dve.wait_ge(rt_exp, h + 1)
                    routed(h, 3, v.tensor_reduce(rm[:, 1, :], rt[:, 1], AX.X, ALU.add))
                    routed(h, 4, v.reciprocal(rm[:, 2, :], rm[:, 1, :]))
                    routed(h, 5, v.tensor_tensor(rt[:, 0], rt[:, 1], per_token(2), ALU.mult))
                    routed(h, 6, v.tensor_reduce(rm[:, 3, :], rt[:, 0], AX.X, ALU.max))
                    routed(h, 7, v.tensor_tensor(rt[:, 5], rt[:, 0], per_token(3), ALU.is_equal))
                elif part == 1:
                    routed(h, 8, v.tensor_tensor(rt[:, 5], rt[:, 5], rank[:, :, :], ALU.mult))
                    routed(h, 9, v.tensor_reduce(rm[:, 9, :], rt[:, 5], AX.X, ALU.max))
                    routed(h, 10, v.tensor_tensor(rt[:, 3], rt[:, 5], per_token(9), ALU.is_equal))
                    routed(h, 11, v.scalar_tensor_tensor(out=rt[:, 2], in0=rt[:, 3], scalar=-2.0, in1=rt[:, 0],
                                                         op0=ALU.mult, op1=ALU.add))
                    routed(h, 12, v.tensor_reduce(rm[:, 4, :], rt[:, 2], AX.X, ALU.max))
                elif part == 2:
                    routed(h, 13, v.tensor_tensor(rt[:, 5], rt[:, 2], per_token(4), ALU.is_equal))
                    routed(h, 14, v.tensor_tensor(rt[:, 5], rt[:, 5], rank[:, :, :], ALU.mult))
                    routed(h, 15, v.tensor_reduce(rm[:, 9, :], rt[:, 5], AX.X, ALU.max))
                    routed(h, 16, v.tensor_tensor(rt[:, 4], rt[:, 5], per_token(9), ALU.is_equal))
                    routed(h, 17, v.tensor_tensor(rt[:, 3], rt[:, 3], rt[:, 4], ALU.add))
                else:
                    routed(h, 18, v.tensor_tensor(rm[:, 5, :], rm[:, 3, :], rm[:, 4, :], ALU.add))
                    routed(h, 19, v.tensor_scalar(rm[:, 6, :], rm[:, 5, :], 1e-12, None, ALU.max))
                    routed(h, 20, v.reciprocal(rm[:, 7, :], rm[:, 6, :]))
                    routed(h, 21, v.tensor_tensor(rt[:, 5], rt[:, 3], rt[:, 0], ALU.mult))
                    routed(h, 22, v.tensor_tensor(rt[:, 4], rt[:, 5], per_token(7), ALU.mult))
                    routed(h, 23, v.tensor_copy(cc[:, :, 0:4:2, :].bitcast(F32R), twice(rt[:, 4])))
                    v.tensor_copy(cc[:, :, 4, :], rt[:, 4])
                    v.tensor_tensor(cc[:, :, 1:4:2, :], twice(rt[:, 4]), cc[:, :, 0:4:2, :],
                                    ALU.subtract).then_inc(comb_ready, 1)

            def low_z(g, b):
                dve.wait_ge(zt_hi, GB * g + b + 1)
                low(zt_part(1, b), bank[ZT_BANK[b]][:, :], zt_part(0, b)).then_inc(zt_lo, 1)

            def add_out(h, b):
                dve.wait_ge(ot_mm, GB * h + b + 1)
                dve.wait_ge(res_ready, h + 1)
                dve.wait_ge(out_stored, 1 + 32 * h)
                v.tensor_tensor(outs[:, b, :, :], bank[OT_BANK[b]][:, :].rearrange("p (t c) -> p t c", c=D),
                                res[:, :, b, :], ALU.add).then_inc(out_add, 1)

            def scale_item(h, i, by_pe):
                dve.wait_ge(gelu_done, ITEMS * h + i + 1)
                if by_pe:
                    dve.wait_ge(rep_mm, i + 1)
                elif i in REP_ITEMS:
                    dve.wait_ge(rep_in[REP_ITEMS.index(i)], 16 * h + 16)
                if i >= 3:
                    wait_low(dve, h, i - 3)
                v.tensor_tensor(scaled[:, i % 3, :], hid[:, i % 2, :], bank[REP_BANK[i % 2]][:, :] if by_pe else rep(i),
                                ALU.mult).then_inc(sc_ready, 1)

            def item_low(h, i):
                dve.wait_ge(sc_hi, ITEMS * h + i + 1)
                low(scs[:, i % RING, 1, :], scaled[:, i % 3, :], scs[:, i % RING, 0, :]).then_inc(sc_lo_dve, 1)

            def norm_x1(g, part):
                if part in (1, 2):
                    if part == 1:
                        dve.wait_ge(x1_add, NT * g + NT)
                    for t in range(4 * part - 4, 4 * part):
                        ln_stats(1, g, x1, t)
                elif part == 3:
                    ln_var(1, g)
                elif 6 <= part < 9:
                    if part == 6:
                        dve.wait_ge(ln_rstd[1], g + 1)
                    for t in range(T * (part - 6) // 3, T * (part - 5) // 3):
                        last = ln_scale(1, z, x1, t)
                    if part == 8:
                        last.then_inc(z_ready, 1)

            def experts(h, g=None, more=False):
                for i in range(ITEMS):
                    scale_item(h, i, g is None and i < REP_PE)
                    if i - 1 in LOW_DVE:
                        item_low(h, i - 1)
                    if g is not None:
                        norm_x1(g, i)
                    if i in (Z_ITEM + 1, Z_ITEM + 2) and g is not None:
                        low_z(g, i - Z_ITEM - 1)
                if ITEMS - 1 in LOW_DVE:
                    item_low(h, ITEMS - 1)
                add_out(h, 0)
                if g is not None:
                    route_start(g)
                if more:
                    for b in range(GB):
                        low_x0t(g + 1, b)
                    route_on(g, 0)
                    low_gt(g + 1, 0, 0)
                elif g is not None:
                    for part in range(4):
                        route_on(g, part)
                add_out(h, 1)
                if more:
                    low_gt(g + 1, 1, 1)
                    route_on(g, 1)
                    low_gt(g + 1, 2, 2)

            def iteration(g, first=False, final=False):
                if not final:
                    for b in range(GB):
                        norm_x_stats(g + 1, b)
                if not first:
                    low_gt(g, 3, 3)

                def low_y2(p):
                    dve.wait_ge(y2_hi, 2 * g + p + 1)
                    low(y2s[:, 1, 2 * p:2 * p + 2], Q[:, 2, 2 * p:2 * p + 2],
                        y2s[:, 0, 2 * p:2 * p + 2]).then_inc(y2_lo, 1)

                if first:
                    dve.wait_ge(wsp_lo, 2)
                else:
                    dve.wait_ge(res_ready, g)
                for i in range(T):
                    b, t = q_tile(i)
                    dve.wait_ge(q_mm, T * g + i + 1)
                    src = bank[GT_BANK[i % 4]][:, 0:BABY * D].rearrange("p (j c) -> p j c", c=D)
                    v.tensor_tensor(Q[:, :, t, b, :], src, bias[:, t], ALU.add).then_inc(q_ready, 1)
                    if not first and i < 2:
                        route_on(g - 1, 2 + i)
                    if not final and i == 2:
                        ln_var(0, g + 1)
                    if not final and i >= 4:
                        norm_x_scale(g + 1, i - 4, 4)
                    if i == T - 3:
                        low_y2(0)
                low_y2(1)

                def low_y1(t):
                    dve.wait_ge(y1_hi, NT * g + t + 1)
                    low(y1s[:, 1, t], y1[:, t], y1s[:, 0, t]).then_inc(y1_lo, 1)

                for t in range(NT):
                    dve.wait_ge(y1_mm, NT * g + t + 1)
                    if t == 0:
                        dve.wait_ge(y2_lo, 2 * g + 2)
                    v.tensor_tensor(y1[:, t], bank[Y1_BANK[t]][:, 0:W].rearrange("p (b c) -> p b c", c=D),
                                    Q[:, 1, t], ALU.add).then_inc(y1_add, 1)
                    if t >= 1:
                        low_y1(t - 1)
                low_y1(NT - 1)
                dve.wait_ge(xq_ready, g + 1)
                for t in range(NT):
                    dve.wait_ge(h8_mm, NT * g + t + 1)
                    v.tensor_tensor(x1[:, t], bank[H8_BANK[t]][:, 0:W].rearrange("p (b c) -> p b c", c=D),
                                    Q[:, 0, t], ALU.add).then_inc(x1_add, 1)
                    if first:
                        dve.wait_ge(x1_add, NT * g + t + 1)
                        for tb in (2 * t, 2 * t + 1):
                            ln_stats(1, g, x1, tb)
                if first:
                    norm_x1(g, 3)
                    for b in range(GB):
                        low_x0t(g + 1, b)
                    for part in range(6, 9):
                        norm_x1(g, part)
                    for k in range(2):
                        low_gt(g + 1, k, k)
                    for b in range(GB):
                        low_z(g, b)
                    low_gt(g + 1, 2, 2)
                    route_start(g)
                    route_on(g, 0)
                    route_on(g, 1)
                else:
                    experts(g - 1, g, not final)

            iteration(0, first=True)
            with dve.Fori(1, GROUPS - 1) as g:
                iteration(g)
            iteration(GROUPS - 1, final=True)
            experts(GROUPS - 1)

        @block.tensor
        def _(pe):
            def mm3(dst, wh, wl, xh, xl, start, stop):
                pe.matmul(dst, wh, xh, start=start, stop=False)
                pe.matmul(dst, wh, xl, start=False, stop=False)
                return pe.matmul(dst, wl, xh, start=False, stop=stop)

            def nodes_product_tile(k, t):
                b, pw = k // 2, k % 2
                last = mm3(bank[GT_BANK[k]][:, :], x0s[:, 0, t, b, :], x0s[:, 1, t, b, :],
                           LT[:, pw, 0, t, :], LT[:, pw, 1, t, :], t == 0, t == NT - 1)
                if t == NT - 1:
                    last.then_inc(gt_mm, 1)

            def nodes_product(k):
                for t in range(NT):
                    nodes_product_tile(k, t)

            def transpose_x0(b, banks=X0_BANK):
                for t in range(NT):
                    last = pe.transpose(bank[banks[b]][:, t * P:(t + 1) * P], x0[:, t, b, :], ident[:, :])
                last.then_inc(x0t_mm, 1)

            def times_powers(dst, left, c):
                first = BABY * c
                if first == 0:
                    pe.matmul(dst[:, 0:D], left, ident[:, :], start=True, stop=True)
                    first = 1
                return pe.matmul(dst[:, (first - BABY * c) * D:BABY * D], left, Rp[:, first - 1:BABY * (c + 1) - 1, :],
                                 start=True, stop=True)

            def power_tile(k, a):
                for t in range(NT):
                    c = slice(a * P, (a + 1) * P)
                    last = mm3(bank[4 + a][:, :], Lns[:, 0, t, c], Lns[:, 1, t, c],
                               LT[:, k - 1, 0, t, :], LT[:, k - 1, 1, t, :], t == 0, t == NT - 1)
                last.then_inc(lt_mm, 1)

            pe.wait_ge(pool_const, 1)
            pe.wait_ge(alpha_in, 16)
            pe.transpose(bank[0][:, 0:NT], alpha_rows[:, :], ident[0:NT, 0:NT]).then_inc(rows_t, 1)
            for t in range(NT):
                pe.wait_ge(lnat_ready, t + 1)
                for a in range(NT):
                    last = pe.transpose(bank[4 + a][:, t * P:(t + 1) * P], Lnat[:, t, a * P:(a + 1) * P], ident[:, :])
                    if t == NT - 1:
                        last.then_inc(lt_mm, 1)
            pe.wait_ge(x0_lo, 1)
            for t in range(NT):
                pe.wait_ge(lt_lo, t + 1)
                nodes_product_tile(0, t)
            pe.wait_ge(rows_in, 64)
            R = E + 2 + E
            pe.transpose(bank[1][:, 2 * P:2 * P + R], rows[:, :], ident[0:R, 0:R]).then_inc(rows_t, 1)
            pe.wait_ge(w_in, 16)
            pe.transpose(bank[1][:, 0:P], w_raw[:, 0, :], ident[:, :]).then_inc(w_t, 1)
            pe.wait_ge(x0_lo, GB)
            nodes_product(2)
            pe.wait_ge(wt_ready, 1)
            pe.matmul(bank[1][:, P:2 * P], wT[:, 1, :], wT[:, 0, :], start=True, stop=True).then_inc(weff_mm, 1)
            for b in range(GB):
                transpose_x0(b, X0_SETUP)
            pe.wait_ge(pow_ready, 1)
            pe.matmul(bank[3][:, 0:P], Rp[:, 0, :], Rp[:, 0, :], start=True, stop=True).then_inc(pow_mm, 1)
            pe.wait_ge(lnat_lo, 1)
            power_tile(1, 0)
            pe.wait_ge(pow_ready, 2)
            pe.matmul(bank[3][:, 0:2 * P], Rp[:, 1, :], Rp[:, 0:2, :], start=True, stop=True).then_inc(pow_mm, 1)
            power_tile(1, 1)
            pe.wait_ge(pow_ready, 3)
            pe.matmul(bank[1][:, :], Rp[:, 3, :], Rp[:, 0:4, :], start=True, stop=True).then_inc(pow_mm, 1)
            pe.wait_ge(x0t_lo, GB)
            power_tile(1, 2)
            pe.wait_ge(pow_ready, 4)
            pe.wait_ge(gt_lo, 1)
            for c in range(BABY):
                times_powers(bank[CREP_BANK[c]], cols[:, FB_COL:FB_COL + 1].to_broadcast([P, P]), c).then_inc(crep_mm, 1)
            power_tile(1, 3)

            def feature_powers(c):
                times_powers(bank[FR_BANK[c]], w_raw[:, 1, :], c).then_inc(fr_mm, 1)

            pe.wait_ge(fc_in, 16)
            pe.wait_ge(crep_ready, 2)
            feature_powers(0)
            pe.wait_ge(gt_lo, 2)
            feature_powers(1)
            pe.wait_ge(lt_lo, 2 * NT)
            pe.wait_ge(crep_ready, BABY)
            nodes_product(1)
            nodes_product(3)
            feature_powers(2)
            for a in range(NT):
                if a == NT - 1:
                    pe.wait_ge(m_sum, BABY)
                power_tile(2, a)
                if a == 0:
                    pe.wait_ge(m_sum, 1)
                    pe.wait_ge(ones_ready, 1)
                    for m in range(NT):
                        for s in range(2):
                            last = pe.matmul(bank[V2_BANK][:, :], ones[:, :], LT[:, 1, s, m, :],
                                             start=(m == 0 and s == 0), stop=(m == NT - 1 and s == 1))
                    last.then_inc(v2_mm, 1)

            def horner(src, banks, done, ready, parts):
                for tiles, count in parts:
                    pe.wait_ge(ready, count)
                    for t in range(NT):
                        yield tiles, t
                        for m in tiles:
                            c = slice(t * P, (t + 1) * P)
                            last = mm3(bank[banks[t]][:, 0:W], LT[:, 2, 0, m, c], LT[:, 2, 1, m, c],
                                       src[:, 0, m], src[:, 1, m], m == 0, m == NT - 1)
                        if tiles[-1] == NT - 1:
                            last.then_inc(done, 1)

            def logits(h):
                pe.wait_ge(zt_lo, GB * h + GB)
                for t in range(T):
                    for s in range(2):
                        c = slice((t // GB) * P, (t // GB + 1) * P)
                        last = pe.matmul(bank[LG_BANK][:, t * C:(t + 1) * C], zt_part(s, t % GB)[:, c], rts[:, :],
                                         start=(s == 0), stop=(s == 1))
                last.then_inc(lg_mm, 1)

            def transpose_comb(h):
                pe.wait_ge(comb_ready, h + 1)
                for t in range(NT):
                    last = pe.transpose(bank[CT_BANK][0:GB * V, t * P:(t + 1) * P],
                                        cc[:, t * GB:(t + 1) * GB, :, :].rearrange("p b k e -> p (b k e)"), ident[:, :])
                last.then_inc(ct_mm, 1)

            def transpose_z(g, b):
                pe.wait_ge(z_ready, g + 1)
                for t in range(NT):
                    last = pe.transpose(bank[ZT_BANK[b]][:, t * P:(t + 1) * P], z[:, t, b, :], ident[:, :])
                last.then_inc(zt_mm, 1)

            def transpose_out(h, b):
                pe.wait_ge(yt_copied, GB * h + b + 1)
                for t in range(NT):
                    last = pe.transpose(bank[OT_BANK[b]][:, t * P:(t + 1) * P], yT[:, t * P:(t + 1) * P], ident[:, :])
                last.then_inc(ot_mm, 1)

            def replicate(h, i):
                if i >= 2:
                    pe.wait_ge(sc_ready, ITEMS * h + i - 1)
                for part in range(2):
                    r = part * E + i
                    last = pe.matmul(bank[REP_BANK[i % 2]][:, :], pick[:, r:r + 1].to_broadcast([GB * V, P]), combT[:, :],
                                     start=part == 0, stop=part == 1)
                last.then_inc(rep_mm, 1)

            def experts(h, g=None, more=False):
                for s in range(ITEMS + LAG):
                    if s < ITEMS:
                        b, e = s // E, s % E
                        if s >= 3:
                            pe.wait_ge(gelu_done, ITEMS * h + s - 2)
                        elif g is not None:
                            pe.wait_ge(x1_add, NT * g + s + 1)
                        elif UP_BANK[s] in OT_BANK:
                            pe.wait_ge(out_add, 1 + GB * h)
                        if s == E:
                            pe.wait_ge(zt_moved, h + 1)
                        mm3(bank[UP_BANK[s % 3]][:, :], w1s[:, 0, e, :], w1s[:, 1, e, :],
                            zT[:, 0, b, :], zT[:, 1, b, :], True, True).then_inc(up_mm, 1)
                        if s == 1 and g is None:
                            transpose_comb(h)
                            pe.wait_ge(ct_high, h + 1)
                            replicate(h, 0)
                        if 1 <= s < REP_PE and g is None:
                            replicate(h, s)
                        if e == LAG - 1:
                            pe.matmul(bank[SUM_BANK[b]][:, :], b2s[:, b, :], combT[:, :], start=True, stop=False)
                    if s == ITEMS and more:
                        pe.wait_ge(x0_ready, g + 2)
                        transpose_x0(0)
                    if s == ITEMS + 1 and more:
                        pe.wait_ge(gelu_done, ITEMS * h + ITEMS - 2)
                        transpose_x0(1)
                    i = s - LAG
                    if i >= 0:
                        b, e = i // E, i % E
                        wait_low(pe, h, i)
                        mm3(bank[SUM_BANK[b]][:, :], w2s[:, 0, e, :], w2s[:, 1, e, :],
                            scs[:, i % RING, 0, :], scs[:, i % RING, 1, :], False, e == E - 1).then_inc(down_mm, 1)
                    if s in (Z_ITEM, Z_ITEM + 1) and g is not None:
                        transpose_z(g, s - Z_ITEM)
                    if s == ITEMS - 1:
                        transpose_out(h, 0)
                        if g is not None:
                            logits(g)
                if more:
                    pe.wait_ge(x0_lo, GB * (g + 1) + GB)
                    pe.wait_ge(out_add, 1 + GB * h + 1)
                    nodes_product(0)
                transpose_out(h, 1)
                if more:
                    nodes_product(1)
                    pe.wait_ge(x0t_lo, GB * g + 2 * GB)
                    nodes_product(2)

            def iteration(g, first=False, final=False):
                if not first:
                    nodes_product(3)
                else:
                    pe.wait_ge(m_lo, 1)
                    pe.wait_ge(v2_read, 1)
                for i in range(T):
                    b, t = q_tile(i)
                    if i in (0, 2):
                        pe.wait_ge(gt_lo, 2 * GB * g + (2 * GB if first else 2 * b + 2))
                    if i >= 4:
                        pe.wait_ge(q_ready, T * g + i - 3)
                    dst = bank[GT_BANK[i % 4]][:, 0:BABY * D]
                    c = slice(t * P, (t + 1) * P)
                    for k in range(BABY):
                        last = mm3(dst, GT[:, b, k, 0, c], GT[:, b, k, 1, c], M[:, 0, :, k, :], M[:, 1, :, k, :],
                                   k == 0, k == BABY - 1)
                    last.then_inc(q_mm, 1)
                    if i == NT - 1 and not first:
                        transpose_comb(g - 1)
                if first:
                    pe.wait_ge(lt_lo, BABY * NT)
                    pe.wait_ge(small_ready, 1)
                for tiles, t in horner(y2s, Y1_BANK, y1_mm, y2_lo, [((0, 1), 2 * g + 1), ((2, 3), 2 * g + 2)]):
                    if tiles[0] == 0:
                        pe.wait_ge(q_ready, T * g + NT + t + 1)
                if not first:
                    pe.wait_ge(ct_high, g)
                for _ in horner(y1s, H8_BANK, h8_mm, y1_lo,
                                [((0,), NT * g + 1), ((1,), NT * g + 2), ((2, 3), NT * g + 4)]):
                    pass
                if first:
                    pe.wait_ge(x0_ready, g + 2)
                    transpose_x0(0)
                    pe.wait_ge(x1_add, NT * g + 2)
                    transpose_x0(1)
                    pe.wait_ge(x0_lo, GB * (g + 2))
                    nodes_product(0)
                    nodes_product(1)
                    transpose_z(g, 0)
                    pe.wait_ge(gt_lo, 2 * GB * (g + 1) + 2)
                    transpose_z(g, 1)
                    pe.wait_ge(x0t_lo, GB * (g + 2))
                    nodes_product(2)
                    logits(g)
                else:
                    experts(g - 1, g, not final)

            iteration(0, first=True)
            with pe.Fori(1, GROUPS - 1) as g:
                iteration(g)
            iteration(GROUPS - 1, final=True)
            experts(GROUPS - 1)


_INS = ['x', 'adj', 'L0_gnn_alpha_train', 'L0_gnn_w', 'L0_gnn_d', 'L0_gnn_fc_in_w', 'L0_gnn_fc_in_b',
        'L0_ffn_router_w', 'L0_ffn_w1', 'L0_ffn_b1', 'L0_ffn_w2', 'L0_ffn_b2']


def kernel(**inputs):
    import numpy as _np
    import concourse.bacc as _bacc
    from concourse import mybir as _mybir
    from concourse.bass_utils import run_bass_kernel_spmd as _run

    nc = _bacc.Bacc("TRN2", target_bir_lowering=False, num_devices=1)
    arrays, args = {}, []
    for name in _INS:
        a = _np.ascontiguousarray(inputs[name])
        arrays[f"in_{name}_dram"] = a
        args.append(nc.dram_tensor(f"in_{name}_dram", a.shape, _mybir.dt.from_np(a.dtype), kind="ExternalInput").ap())
    shape = arrays["in_x_dram"].shape
    E, (B, N) = inputs["L0_ffn_router_w"].shape[0], shape[0:2]
    args.append(nc.dram_tensor("comb_rows", (B // 2, 2, E, N), _mybir.dt.float32, kind="Internal").ap())
    args.append(nc.dram_tensor("out_0_dram", shape, _mybir.dt.float32, kind="ExternalOutput").ap())
    build(nc, *args)
    r = _run(nc, [arrays], core_ids=[0])
    return r.results[0]["out_0_dram"]
```
